# Optimizing a Trainium2 kernel written in Bass

```python
import numpy as np
import jax
import jax.numpy as jnp

def _softmax(x, axis=-1):
    return jax.nn.softmax(x, axis=axis)

def _gelu(x):
    return jax.nn.gelu(x, approximate=True)

def _silu(x):
    return jax.nn.silu(x)

def _sigmoid(x):
    return jax.nn.sigmoid(x)

def _layernorm(x, axis=-1, eps=1e-05):
    m = jnp.mean(x, axis=axis, keepdims=True)
    v = jnp.var(x, axis=axis, keepdims=True)
    return (x - m) / jnp.sqrt(v + eps)

def _scatter_add(tgt, idx, src, axis=0):
    return tgt.at[idx].add(src)

def _segment_sum(src, seg, n):
    return jax.ops.segment_sum(src, seg, n)
kernel_name = 'mk_adj_resnorm_d2_adj_r2_8cf2d1'

def setup_inputs(seed: int=0):
    np.random.seed(seed)
    _w = jnp.asarray

    def _rec_inputs():
        import jax
        import jax.numpy as jnp
        _gk = jax.random.key(seed)
        x = 7.22e-05 + 1 * jax.random.normal(jax.random.fold_in(_gk, 1), (16, 512, 256), jnp.float32)
        _a = jax.random.bernoulli(jax.random.fold_in(_gk, 2), 0.015625, (16, 512, 512))
        _a = jnp.logical_or(_a, jnp.swapaxes(_a, -1, -2))
        _a = jnp.logical_or(_a, jnp.eye(512, dtype=bool))
        adj = _a.astype(jnp.int32)
        return (x, adj)
    x, adj = _rec_inputs()

    def _L0_gnn_setup():
        import jax, jax.numpy as jnp
        import numpy as np
        ALPHA = 0.2
        NEG_INF = -1000000000.0
        key = jax.random.key(seed)
        k1, k2, k3, k4 = jax.random.split(key, 4)
        B, N, IN, OUT = (8, 1024, 256, 32)
        graph_input = jax.random.normal(k1, (B, N, IN), dtype=jnp.float32)
        adj = jax.random.randint(k2, (B, N, N), 0, 2, dtype=jnp.int32)
        W_fc = jax.random.normal(k3, (OUT, IN), dtype=jnp.float32) * (1.0 / np.sqrt(IN))
        W_attn = jax.random.normal(k4, (1, 2 * OUT), dtype=jnp.float32) * (1.0 / np.sqrt(2 * OUT))
        return {'graph_input': graph_input, 'adj': adj, 'W_fc': W_fc, 'W_attn': W_attn}
    _L0_gnn_all = _L0_gnn_setup()
    _L0_gnn_in = {k: v for k, v in _L0_gnn_all.items() if k in ('W_fc', 'W_attn')}
    del _L0_gnn_all

    def _L1_gnn_setup():
        import jax, jax.numpy as jnp
        import numpy as np
        EPS = 1e-12
        key = jax.random.key(seed)
        k1, k2 = jax.random.split(key)
        B, T, D = (8, 1024, 256)
        x = jax.random.normal(k1, (B, T, D), dtype=jnp.float32)
        adj = jax.random.randint(k2, (B, T, T), 0, 2, dtype=jnp.int32)
        return {'x': x, 'adj': adj}
    _L1_gnn_all = _L1_gnn_setup()
    _L1_gnn_in = {k: v for k, v in _L1_gnn_all.items() if k in ()}
    del _L1_gnn_all
    return {'x': x, 'adj': adj, 'L0_gnn_W_fc': _L0_gnn_in['W_fc'], 'L0_gnn_W_attn': _L0_gnn_in['W_attn']}

def reference(x, adj, L0_gnn_W_fc, L0_gnn_W_attn):
    import jax
    import jax.numpy as jnp

    def _L0_gnn_ref(graph_input, adj, W_fc, W_attn):
        import jax, jax.numpy as jnp
        import numpy as np
        ALPHA = 0.2
        NEG_INF = -1000000000.0
        h = jnp.einsum('bni,oi->bno', graph_input, W_fc)
        out_dim = W_fc.shape[0]
        a1 = W_attn[0, :out_dim]
        a2 = W_attn[0, out_dim:]
        f1 = jnp.einsum('bno,o->bn', h, a1)
        f2 = jnp.einsum('bno,o->bn', h, a2)
        scores = jax.nn.leaky_relu(f1[:, :, None] + f2[:, None, :], negative_slope=ALPHA)
        scores = jnp.where(adj == 0, NEG_INF, scores)
        attn = jax.nn.softmax(scores, axis=2)
        h_prime = jnp.einsum('bnm,bmi->bni', attn, graph_input)
        return jax.nn.elu(h_prime)

    def _L1_gnn_ref(x, adj):
        import jax, jax.numpy as jnp
        import numpy as np
        EPS = 1e-12
        a_d = adj.astype(jnp.float32)
        nrm = jnp.sqrt(jnp.maximum(jnp.sum(x * x, axis=-1, keepdims=True), EPS))
        xn = x / nrm
        a_s = jnp.einsum('btd,bsd->bts', xn, xn)
        a = jnp.einsum('bts,bsr->btr', a_s, a_d)
        out = jnp.einsum('btr,brd->btd', a, x)
        return out
    x = _layernorm(x + _L0_gnn_ref(x, adj, L0_gnn_W_fc, L0_gnn_W_attn), axis=-1)
    x = _layernorm(x + _L1_gnn_ref(x, adj), axis=-1)
    return x

_drawn_inputs = setup_inputs


def setup_inputs(seed=0):
    import zlib

    import numpy as np

    out = dict(_drawn_inputs(seed))
    spreads = {}
    factors = {}
    for name, (base, spread) in spreads.items():
        noise = np.random.default_rng([zlib.crc32(name.encode()), seed]).standard_normal(out[name].shape)
        drawn = base * np.exp(spread * noise) if base else spread * noise
        out[name] = jnp.asarray(drawn.astype(out[name].dtype))
    for name, factor in factors.items():
        out[name] = (out[name] * factor).astype(out[name].dtype)
    return out
```

```python
from contextlib import ExitStack

import numpy as np

import concourse.bass as bass
from concourse import mybir

F32 = mybir.dt.float32
F32R = mybir.dt.float32r
BF16 = mybir.dt.bfloat16
ACT = mybir.ActivationFunctionType
ALU = mybir.AluOpType

P = 128
SLOPE = 0.2
MASKED = -1e30
LOWEST = -3e38
LN_EPS = 1e-5
NORM_EPS = 1e-12
NBUF = 3


def program(nc, x, adj, w_fc, w_attn, out):
    B, N, D = x.shape
    O = w_fc.shape[0]
    NC = N // P
    DC = D // P
    HEAD = 2
    LOOPS = (B - 1 - HEAD) // NBUF
    TAIL = HEAD + LOOPS * NBUF

    x_rows = x.rearrange("b (c p) d -> b p c d", p=P)
    adj_rows = adj.rearrange("b (c p) m -> b p c m", p=P)
    out_rows = out.rearrange("b (c p) d -> b p c d", p=P)

    with ExitStack() as ctx:
        def sb(name, shape, dt):
            return ctx.enter_context(nc.sbuf_tensor(name, shape, dt))

        def psum(name):
            return ctx.enter_context(nc.psum_tensor(name, [P, 512], F32))

        def sem(name):
            return ctx.enter_context(nc.semaphore(name))

        ident = sb("ident", [P, P], F32)
        minus_half = sb("minus_half", [P, NC], F32)
        wfc = sb("wfc", [O, D], F32)
        attn_cols = sb("attn_cols", [O, 2], F32)
        attn_wide = sb("attn_wide", [O, 2, P], F32)
        v_bcast = sb("v_bcast", [P, 2, D], F32)
        x_sb = [sb(f"x_sb{n}", [P, NC, D], F32) for n in range(NBUF)]
        x_hi = [sb(f"x_hi{n}", [P, NC, D], F32R) for n in range(NBUF)]
        x_lo = [sb(f"x_lo{n}", [P, NC, D], F32R) for n in range(NBUF)]
        adj_sb = [sb(f"adj_sb{n}", [P, NC, N], F32R) for n in range(NBUF)]
        xn = [sb(f"xn{n}", [P, NC, D], F32) for n in range(NBUF)]
        xn_hi = [sb(f"xn_hi{n}", [P, NC, D], F32R) for n in range(NBUF)]
        xn_lo = [sb(f"xn_lo{n}", [P, NC, D], F32R) for n in range(NBUF)]
        nrm = [sb(f"nrm{n}", [P, NC], F32) for n in range(NBUF)]
        f = [sb(f"f{n}", [P, 2, NC], F32) for n in range(NBUF)]
        neg_max = [sb(f"neg_max{n}", [P, NC], F32) for n in range(NBUF)]
        den = [sb(f"den{n}", [P, NC], F32) for n in range(NBUF)]
        rden = [sb(f"rden{n}", [P, NC], F32) for n in range(NBUF)]
        mask = sb("mask", [P, NC, N], BF16)
        f2_small = sb("f2_small", [P, N], F32)
        slope_mask = sb("slope_mask", [P, NC, N], F32)
        score_sb = sb("score_sb", [P, NC, N], F32)
        prob = sb("prob", [P, NC, N], F32)
        probT_hi = sb("probT_hi", [P, NC, N], F32R)
        probT_lo = sb("probT_lo", [P, NC, N], F32R)
        exp_h = sb("exp_h", [P, NC, D], F32)
        relu_h = sb("relu_h", [P, NC, D], F32)
        z_hi = sb("z_hi", [P, NC, D], F32R)
        z_lo = sb("z_lo", [P, NC, D], F32R)
        xnT_hi = sb("xnT_hi", [P, DC, N], F32R)
        xnT_lo = sb("xnT_lo", [P, DC, N], F32R)
        w_hi = sb("w_hi", [P, DC, D], F32R)
        w_lo = sb("w_lo", [P, DC, D], F32R)
        y2 = sb("y2", [P, NC, D], F32)
        o_sb = sb("o_sb", [P, NC, D], F32)
        product = sb("product", [P, D], F32)
        row_max = sb("row_max", [P, NC], F32)
        stats = sb("stats", [P, NC, 6], F32)
        mv = sb("mv", [P, NC, 2], F32)
        stats2 = sb("stats2", [P, NC, 6], F32)
        mv2 = sb("mv2", [P, NC, 2], F32)
        ve = sb("ve", [P, NC], F32)
        rstd = sb("rstd", [P, NC], F32)
        rstd_sq = sb("rstd_sq", [P, NC], F32)
        ss = sb("ss", [P, NC], F32)
        ss_floor = sb("ss_floor", [P, NC], F32)
        rnrm = sb("rnrm", [P, NC], F32)
        xn_scale = sb("xn_scale", [P, NC], F32)
        ve2 = sb("ve2", [P, NC], F32)
        rstd2 = sb("rstd2", [P, NC], F32)

        ps_f2 = psum("ps_f2")
        ps_probT = [psum(f"ps_probT{n}") for n in range(2)]
        ps_h = [psum(f"ps_h{n}") for n in range(2)]
        ps_l1 = [psum(f"ps_l1_{n}") for n in range(3)]
        Z0, XT0, W0, O0 = 0, NC, NC + DC, NC + 2 * DC
        TILES = 2 * NC + 2 * DC
        assert TILES % 3 == 0

        wfc_in = sem("wfc_in")
        x_in = [sem(f"x_in{n}") for n in range(NBUF)]
        adj_in = [sem(f"adj_in{n}") for n in range(NBUF)]
        out_stored = sem("out_stored")
        consts = sem("consts")
        attn_wide_ok = sem("attn_wide_ok")
        ps_v_ok = sem("ps_v_ok")
        v_ok = sem("v_ok")
        f_part = sem("f_part")
        x_hi_ok = sem("x_hi_ok")
        x_lo_ok = sem("x_lo_ok")
        f2_bcast = sem("f2_bcast")
        mask_ok = sem("mask_ok")
        score_ok = sem("score_ok")
        slope_mask_ok = sem("slope_mask_ok")
        neg_max_ok = sem("neg_max_ok")
        f2_small_ok = sem("f2_small_ok")
        relu_z_ok = sem("relu_z_ok")
        prob_ok = sem("prob_ok")
        rden_ok = sem("rden_ok")
        probT_ps = sem("probT_ps")
        probT_hi_ok = sem("probT_hi_ok")
        probT_lo_ok = sem("probT_lo_ok")
        h_ps = sem("h_ps")
        elu_ok = sem("elu_ok")
        q_ok = sem("q_ok")
        y_ok = sem("y_ok")
        stats_ok = sem("stats_ok")
        mv_ok = sem("mv_ok")
        norm_step = sem("norm_step")
        norm_ok = sem("norm_ok")
        xn_ok = sem("xn_ok")
        xn_hi_ok = sem("xn_hi_ok")
        xn_lo_ok = sem("xn_lo_ok")
        z_ps = sem("z_ps")
        z_hi_ok = sem("z_hi_ok")
        z_lo_ok = sem("z_lo_ok")
        xnT_ps = sem("xnT_ps")
        xnT_hi_ok = sem("xnT_hi_ok")
        xnT_lo_ok = sem("xnT_lo_ok")
        w_ps = sem("w_ps")
        w_hi_ok = sem("w_hi_ok")
        w_lo_ok = sem("w_lo_ok")
        o_ps = sem("o_ps")
        y2_ok = sem("y2_ok")
        stats2_ok = sem("stats2_ok")
        mv2_ok = sem("mv2_ok")
        ve2_ok = sem("ve2_ok")
        rstd2_ok = sem("rstd2_ok")
        o_ok = sem("o_ok")

        block = ctx.enter_context(nc.Block())

        def run_steps(eng, step):
            for i in range(HEAD):
                step(i, i // NBUF, i % NBUF, i > 0, True)
            with eng.Fori(0, LOOPS) as j:
                for u in range(NBUF):
                    step(j * NBUF + (HEAD + u), j + (HEAD + u) // NBUF, (HEAD + u) % NBUF, True, True)
            for i in range(TAIL, B):
                step(i, i // NBUF, i % NBUF, True, i + 1 < B)
            step(B, B // NBUF, B % NBUF, True, False)

        def is_graph(i):
            return not isinstance(i, int) or i < B

        @block.sync
        def _(sp):
            def load_x(i, n):
                sp.dma_start(x_sb[n][:], x_rows[i]).then_inc(x_in[n], 16)

            sp.dma_start(wfc[:], w_fc).then_inc(wfc_in, 16)
            for k in range(2):
                sp.dma_start(attn_cols[:, k:k + 1], w_attn[0, k * O:(k + 1) * O].rearrange("(o u) -> o u", u=1),
                             ).then_inc(wfc_in, 16)
            load_x(0, 0)
            load_x(1, 1)

            def step(i, r, n, layer1, prep):
                if (i + 2 < B) if isinstance(i, int) else True:
                    if layer1:
                        sp.wait_ge(y_ok, i)
                    load_x(i + 2, (n + 2) % NBUF)
                if layer1:
                    sp.wait_ge(o_ok, i)
                    sp.dma_start(out_rows[i - 1], o_sb[:]).then_inc(out_stored, 16)

            run_steps(sp, step)
            sp.wait_ge(out_stored, 16 * B)

        @block.gpsimd
        def _(pool):
            def load_adj(i, n):
                pool.dma_start(adj_sb[n][:], adj_rows[i]).then_inc(adj_in[n], 16)

            load_adj(0, 0)
            load_adj(1, 1)
            pool.memset(ident[:], 0.0).then_inc(consts, 1)
            pool.memset(minus_half[:], -0.5).then_inc(consts, 1)
            pool.wait_ge(consts, 2)
            pool.affine_select(out=ident[:], in_=ident[:], compare_op=ALU.not_equal, fill=1.0, base=0,
                               pattern=[[-1, P]], channel_multiplier=1).then_inc(consts, 1)
            pool.wait_ge(consts, 3)

            def split_x(i, n):
                pool.wait_ge(x_hi_ok, i + 1)
                pool.tensor_tensor(x_lo[n][:], x_sb[n][:], x_hi[n][:].bitcast(F32),
                                   ALU.subtract).then_inc(x_lo_ok, 1)

            def mask_part(i, c):
                if c == 0:
                    pool.wait_ge(f2_small_ok, i + 1)
                    pool.wait_ge(mask_ok, i + 1)
                if not isinstance(i, int) or i > 0:
                    pool.wait_ge(score_ok, NC * (i - 1) + c + 1)
                pool.tensor_tensor(slope_mask[:, c, :], f2_small[:], mask[:, c, :], ALU.add).then_inc(slope_mask_ok, 1)

            split_x(0, 0)
            for c in range(NC):
                mask_part(0, c)

            def step(i, r, n, layer1, prep):
                if (i + 2 < B) if isinstance(i, int) else True:
                    if layer1:
                        pool.wait_ge(z_ps, NC * i)
                    load_adj(i + 2, (n + 2) % NBUF)
                if prep:
                    split_x(i + 1, (n + 1) % NBUF)
                    for c in range(NC):
                        mask_part(i + 1, c)
                if is_graph(i):
                    pool.wait_ge(mv_ok, i + 1)
                    pool.nop(nofuse=True)
                    pool.tensor_scalar(ve[:], mv[:, :, 1], LN_EPS, 1.0, ALU.add, ALU.mult).then_inc(norm_step, 1)
                    pool.wait_ge(norm_step, 7 * i + 1)
                    pool.tensor_tensor(rstd[:], ve[:], minus_half[:], ALU.pow).then_inc(norm_step, 1)
                    pool.wait_ge(norm_step, 7 * i + 2)
                    pool.tensor_tensor(rstd_sq[:], rstd[:], rstd[:], ALU.mult).then_inc(norm_step, 1)
                    pool.wait_ge(norm_step, 7 * i + 3)
                    pool.tensor_tensor(ss[:], rstd_sq[:], mv[:, :, 1], ALU.mult).then_inc(norm_step, 1)
                    pool.wait_ge(norm_step, 7 * i + 4)
                    pool.nop(nofuse=True)
                    pool.tensor_scalar(ss_floor[:], ss[:], float(D), NORM_EPS, ALU.mult, ALU.max).then_inc(norm_step, 1)
                    pool.wait_ge(norm_step, 7 * i + 5)
                    pool.tensor_tensor(rnrm[:], ss_floor[:], minus_half[:], ALU.pow).then_inc(norm_step, 1)
                    pool.wait_ge(norm_step, 7 * i + 6)
                    if layer1:
                        pool.wait_ge(xn_ok, i)
                    pool.tensor_tensor(xn_scale[:], rstd[:], rnrm[:], ALU.mult).then_inc(norm_step, 1)
                    pool.tensor_tensor(nrm[n][:], ss_floor[:], rnrm[:], ALU.mult).then_inc(norm_ok, 1)
                    pool.wait_ge(xn_hi_ok, i + 1)
                    pool.tensor_tensor(xn_lo[n][:], xn[n][:], xn_hi[n][:].bitcast(F32),
                                       ALU.subtract).then_inc(xn_lo_ok, 1)
                if layer1:
                    pool.wait_ge(mv2_ok, i)
                    pool.nop(nofuse=True)
                    pool.tensor_scalar(ve2[:], mv2[:, :, 1], LN_EPS, 1.0, ALU.add, ALU.mult).then_inc(ve2_ok, 1)
                    pool.wait_ge(ve2_ok, i)
                    pool.tensor_tensor(rstd2[:], ve2[:], minus_half[:], ALU.pow).then_inc(rstd2_ok, 1)

            run_steps(pool, step)

        @block.vector
        def _(dve):
            dve.wait_ge(wfc_in, 48)
            for k in range(2):
                last = nc.vector.tensor_copy(attn_wide[:, k, :], attn_cols[:, k:k + 1].to_broadcast([O, P]))
            last.then_inc(attn_wide_ok, 1)
            dve.wait_ge(ps_v_ok, 1)
            nc.vector.tensor_scalar(v_bcast[:, 0, :], ps_f2[:, 0:D], 1.0 - SLOPE, None, ALU.mult).then_inc(v_ok, 1)
            nc.vector.tensor_copy(v_bcast[:, 1, :], ps_f2[:, D:2 * D]).then_inc(v_ok, 1)
            dve.wait_ge(v_ok, 2)

            def node_scores(i, r, n):
                dve.wait_ge(x_in[n], 16 * (r + 1))
                for k in range(2):
                    for c in range(NC):
                        nc.vector.tensor_tensor_reduce(
                            out=product[:], in0=x_sb[n][:, c, :], in1=v_bcast[:, k, :], scale=1.0, scalar=0.0,
                            op0=ALU.mult, op1=ALU.add, accum_out=f[n][:, k, c:c + 1]).then_inc(f_part, 1)
                        dve.wait_ge(f_part, 2 * NC * i + NC * k + c + 1)

            def split_x_hi(i, n):
                nc.vector.tensor_copy(x_hi[n][:], x_sb[n][:]).then_inc(x_hi_ok, 1)

            def make_mask(i, r, n):
                dve.wait_ge(adj_in[n], 16 * (r + 1))
                if not isinstance(i, int) or i > 0:
                    dve.wait_ge(slope_mask_ok, NC * i)
                nc.vector.tensor_scalar(mask[:], adj_sb[n][:].bitcast(F32), 0.0, MASKED,
                                        ALU.is_equal, ALU.mult).then_inc(mask_ok, 1)

            def score(i, n, c):
                dve.wait_ge(relu_z_ok, NC * i + c + 1)
                dve.wait_ge(slope_mask_ok, NC * i + c + 1)
                dve.nop(nofuse=True)
                nc.vector.tensor_tensor_reduce(
                    out=score_sb[:, c, :], in0=score_sb[:, c, :], in1=slope_mask[:, c, :], scale=1.0, scalar=LOWEST,
                    op0=ALU.add, op1=ALU.max, accum_out=row_max[:, c:c + 1]).then_inc(score_ok, 1)

            def negate_max(i, n):
                dve.wait_ge(score_ok, NC * (i + 1))
                nc.vector.tensor_scalar(neg_max[n][:], row_max[:], -1.0, None, ALU.mult).then_inc(neg_max_ok, 1)

            def probT_lo_part(i, c):
                dve.wait_ge(probT_hi_ok, NC * i + c + 1)
                nc.vector.tensor_tensor(probT_lo[:, c, :], ps_probT[c % 2][:], probT_hi[:, c, :].bitcast(F32),
                                        ALU.subtract).then_inc(probT_lo_ok, 1)

            def residual(i, n):
                dve.wait_ge(elu_ok, NC * (i + 1))
                nc.vector.scalar_tensor_tensor(out=exp_h[:], in0=exp_h[:], scalar=1.0, in1=x_sb[n][:],
                                               op0=ALU.min, op1=ALU.add).then_inc(q_ok, 1)
                dve.wait_ge(q_ok, i + 1)
                nc.vector.tensor_tensor(relu_h[:], relu_h[:], exp_h[:], ALU.add).then_inc(y_ok, 1)

            def row_stats(i, n):
                dve.wait_ge(y_ok, i + 1)
                for c in range(NC):
                    nc.vector.bn_stats(stats[:, c, :], relu_h[:, c, :]).then_inc(stats_ok, 1)
                if not isinstance(i, int) or i > 0:
                    dve.wait_ge(norm_ok, i)
                dve.wait_ge(stats_ok, NC * (i + 1))
                dve.nop(nofuse=True)
                for c in range(NC):
                    last = nc.vector.bn_aggr(mv[:, c, :], stats[:, c, :])
                last.then_inc(mv_ok, 1)

            def normalise(i, n):
                dve.wait_ge(mv_ok, i + 1)
                dve.wait_ge(norm_ok, i + 1)
                for c in range(NC):
                    last = nc.vector.tensor_scalar(xn[n][:, c, :], relu_h[:, c, :], mv[:, c, 0:1],
                                                   xn_scale[:, c:c + 1], ALU.subtract, ALU.mult)
                last.then_inc(xn_ok, 1)

            def z_lo_part(b, n, c):
                dve.wait_ge(z_hi_ok, NC * b + c + 1)
                nc.vector.scalar_tensor_tensor(out=z_lo[:, c, :], in0=ps_l1[(Z0 + c) % 3][:, 0:D],
                                               scalar=nrm[n][:, c:c + 1], in1=z_hi[:, c, :].bitcast(F32),
                                               op0=ALU.mult, op1=ALU.subtract).then_inc(z_lo_ok, 1)

            def xnT_lo_part(b, d):
                dve.wait_ge(xnT_hi_ok, DC * b + d + 1)
                nc.vector.tensor_tensor(xnT_lo[:, d, :], ps_l1[(XT0 + d) % 3][:], xnT_hi[:, d, :].bitcast(F32),
                                        ALU.subtract).then_inc(xnT_lo_ok, 1)

            def w_lo_part(b, d):
                dve.wait_ge(w_hi_ok, DC * b + d + 1)
                nc.vector.tensor_tensor(w_lo[:, d, :], ps_l1[(W0 + d) % 3][:, 0:D], w_hi[:, d, :].bitcast(F32),
                                        ALU.subtract).then_inc(w_lo_ok, 1)

            def residual2(b, n, c):
                dve.wait_ge(o_ps, NC * b + c + 1)
                nc.vector.scalar_tensor_tensor(out=y2[:, c, :], in0=xn[n][:, c, :], scalar=nrm[n][:, c:c + 1],
                                               in1=ps_l1[(O0 + c) % 3][:, 0:D],
                                               op0=ALU.mult, op1=ALU.add).then_inc(y2_ok, 1)

            def row_stats2(b):
                for c in range(NC):
                    dve.wait_ge(y2_ok, NC * b + c + 1)
                    nc.vector.bn_stats(stats2[:, c, :], y2[:, c, :]).then_inc(stats2_ok, 1)
                dve.wait_ge(stats2_ok, NC * (b + 1))
                dve.nop(nofuse=True)
                for c in range(NC):
                    last = nc.vector.bn_aggr(mv2[:, c, :], stats2[:, c, :])
                last.then_inc(mv2_ok, 1)

            def normalise2(b, i):
                dve.wait_ge(mv2_ok, b + 1)
                dve.wait_ge(rstd2_ok, b + 1)
                if not isinstance(b, int) or b > 0:
                    dve.wait_ge(out_stored, 16 * b)
                for c in range(NC):
                    last = nc.vector.tensor_scalar(o_sb[:, c, :], y2[:, c, :], mv2[:, c, 0:1],
                                                   rstd2[:, c:c + 1], ALU.subtract, ALU.mult)
                last.then_inc(o_ok, 1)

            node_scores(0, 0, 0)
            split_x_hi(0, 0)
            make_mask(0, 0, 0)
            for c in range(NC):
                score(0, 0, c)
            negate_max(0, 0)

            def step(i, r, n, layer1, prep):
                m, l = (n + 1) % NBUF, (n - 1) % NBUF
                if is_graph(i):
                    dve.wait_ge(prob_ok, NC * (i + 1))
                    nc.vector.reciprocal(rden[n][:], den[n][:]).then_inc(rden_ok, 1)
                    probT_lo_part(i, 0)
                if prep:
                    node_scores(i + 1, r + (n + 1) // NBUF, m)
                if is_graph(i):
                    probT_lo_part(i, 1)
                    probT_lo_part(i, 2)
                if prep:
                    split_x_hi(i + 1, m)
                    make_mask(i + 1, r + (n + 1) // NBUF, m)
                if is_graph(i):
                    probT_lo_part(i, 3)
                for c in range(NC):
                    if layer1:
                        z_lo_part(i - 1, l, c)
                    if prep:
                        score(i + 1, m, c)
                if prep:
                    negate_max(i + 1, m)
                if layer1:
                    for d in range(DC):
                        xnT_lo_part(i - 1, d)
                if is_graph(i):
                    residual(i, n)
                if layer1:
                    for d in range(DC):
                        w_lo_part(i - 1, d)
                if is_graph(i):
                    row_stats(i, n)
                if layer1:
                    for c in range(NC):
                        residual2(i - 1, l, c)
                if is_graph(i):
                    normalise(i, n)
                if layer1:
                    row_stats2(i - 1)
                    normalise2(i - 1, i)

            run_steps(dve, step)

        @block.scalar
        def _(act):
            def small_f2(i):
                act.wait_ge(f2_bcast, i + 1)
                if not isinstance(i, int) or i > 0:
                    act.wait_ge(slope_mask_ok, NC * i)
                nc.scalar.activation(f2_small[:], ps_f2[:], ACT.Copy, scale=SLOPE).then_inc(f2_small_ok, 1)

            def relu_z(i, n, c):
                if c == 0:
                    act.wait_ge(f2_bcast, i + 1)
                    if not isinstance(i, int) or i > 0:
                        act.wait_ge(prob_ok, NC * i)
                nc.scalar.activation(score_sb[:, c, :], ps_f2[:], ACT.Relu, bias=f[n][:, 0, c:c + 1],
                                     scale=1.0 - SLOPE).then_inc(relu_z_ok, 1)

            def softmax_exp(i, n, c):
                if c == 0:
                    act.wait_ge(neg_max_ok, i + 1)
                if not isinstance(i, int) or i > 0:
                    act.wait_ge(probT_ps, NC * (i - 1) + c + 1)
                nc.scalar.activation(prob[:, c, :], score_sb[:, c, :], ACT.Exp, bias=neg_max[n][:, c:c + 1],
                                     accum_out=den[n][:, c:c + 1]).then_inc(prob_ok, 1)

            def probT_hi_part(i, c):
                act.wait_ge(probT_ps, NC * i + c + 1)
                if not isinstance(i, int) or i > 0:
                    act.wait_ge(h_ps, NC * (i - 1) + c + 1)
                nc.scalar.activation(probT_hi[:, c, :], ps_probT[c % 2][:], ACT.Copy).then_inc(probT_hi_ok, 1)

            def elu_parts(i, n, c):
                if c == 0:
                    act.wait_ge(rden_ok, i + 1)
                    if not isinstance(i, int) or i > 0:
                        act.wait_ge(xn_ok, i)
                act.wait_ge(h_ps, NC * i + c + 1)
                nc.scalar.activation(exp_h[:, c, :], ps_h[c % 2][:, 0:D], ACT.Exp, scale=rden[n][:, c:c + 1])
                nc.scalar.activation(relu_h[:, c, :], ps_h[c % 2][:, 0:D], ACT.Relu,
                                     scale=rden[n][:, c:c + 1]).then_inc(elu_ok, 1)

            def xn_hi_part(i, n):
                act.wait_ge(xn_ok, i + 1)
                nc.scalar.activation(xn_hi[n][:], xn[n][:], ACT.Copy).then_inc(xn_hi_ok, 1)

            def z_hi_part(b, n, c):
                act.wait_ge(z_ps, NC * b + c + 1)
                if c == 0 and (not isinstance(b, int) or b > 0):
                    act.wait_ge(w_ps, DC * b)
                nc.scalar.activation(z_hi[:, c, :], ps_l1[(Z0 + c) % 3][:, 0:D], ACT.Copy,
                                     scale=nrm[n][:, c:c + 1]).then_inc(z_hi_ok, 1)

            def xnT_hi_part(b, d):
                act.wait_ge(xnT_ps, DC * b + d + 1)
                nc.scalar.activation(xnT_hi[:, d, :], ps_l1[(XT0 + d) % 3][:], ACT.Copy).then_inc(xnT_hi_ok, 1)

            def w_hi_part(b, d):
                act.wait_ge(w_ps, DC * b + d + 1)
                nc.scalar.activation(w_hi[:, d, :], ps_l1[(W0 + d) % 3][:, 0:D], ACT.Copy).then_inc(w_hi_ok, 1)

            small_f2(0)
            for c in range(NC):
                relu_z(0, 0, c)
            for c in range(NC):
                softmax_exp(0, 0, c)

            def step(i, r, n, layer1, prep):
                m, l = (n + 1) % NBUF, (n - 1) % NBUF
                if is_graph(i):
                    probT_hi_part(i, 0)
                    probT_hi_part(i, 1)
                    probT_hi_part(i, 2)
                    elu_parts(i, n, 0)
                    probT_hi_part(i, 3)
                    elu_parts(i, n, 1)
                    elu_parts(i, n, 2)
                    elu_parts(i, n, 3)
                if prep:
                    small_f2(i + 1)
                for c in range(NC):
                    if prep:
                        relu_z(i + 1, m, c)
                    if layer1:
                        z_hi_part(i - 1, l, c)
                if layer1:
                    for d in range(DC):
                        xnT_hi_part(i - 1, d)
                if prep:
                    softmax_exp(i + 1, m, 0)
                    softmax_exp(i + 1, m, 1)
                if layer1:
                    w_hi_part(i - 1, 0)
                if prep:
                    softmax_exp(i + 1, m, 2)
                if layer1:
                    w_hi_part(i - 1, 1)
                if prep:
                    softmax_exp(i + 1, m, 3)
                if is_graph(i):
                    xn_hi_part(i, n)

            run_steps(act, step)

        @block.tensor
        def _(pe):
            pe.wait_ge(attn_wide_ok, 1)
            for k in range(2):
                last = nc.tensor.matmul(ps_f2[:, k * D:(k + 1) * D], attn_wide[:, k, :], wfc[:], start=True, stop=True)
            last.then_inc(ps_v_ok, 1)

            def bcast_f2(i, n):
                pe.wait_ge(f_part, 2 * NC * (i + 1))
                if isinstance(i, int) and i == 0:
                    pe.wait_ge(v_ok, 2)
                    pe.wait_ge(consts, 3)
                else:
                    pe.wait_ge(relu_z_ok, NC * i)
                for c in range(NC):
                    last = nc.tensor.transpose(ps_f2[:, c * P:(c + 1) * P],
                                               f[n][:, 1, c:c + 1].to_broadcast([P, P]), ident[:])
                last.then_inc(f2_bcast, 1)

            def transpose_prob(i, c):
                pe.wait_ge(prob_ok, NC * i + c + 1)
                if c >= 2:
                    pe.wait_ge(probT_lo_ok, NC * i + c - 1)
                elif not isinstance(i, int) or i > 0:
                    pe.wait_ge(probT_lo_ok, NC * i + c - 1)
                for k in range(NC):
                    last = nc.tensor.transpose(ps_probT[c % 2][:, k * P:(k + 1) * P],
                                               prob[:, c, k * P:(k + 1) * P], ident[:])
                last.then_inc(probT_ps, 1)

            def attend(i, n, c):
                pe.wait_ge(probT_lo_ok, NC * i + c + 1)
                if c == 0:
                    pe.wait_ge(x_lo_ok, i + 1)
                if c >= 2 or not isinstance(i, int) or i > 0:
                    pe.wait_ge(elu_ok, NC * i + c - 1)
                for k in range(NC):
                    blk = slice(k * P, (k + 1) * P)
                    ps = ps_h[c % 2][:, 0:D]
                    nc.tensor.matmul(ps, probT_hi[:, c, blk], x_hi[n][:, k, :], start=(k == 0), stop=False)
                    nc.tensor.matmul(ps, probT_hi[:, c, blk], x_lo[n][:, k, :], start=False, stop=False)
                    last = nc.tensor.matmul(ps, probT_lo[:, c, blk], x_hi[n][:, k, :], start=False,
                                            stop=(k == NC - 1))
                last.then_inc(h_ps, 1)

            def bank_free(b, t):
                if t >= 3:
                    u = t - 3
                    g = b
                else:
                    u = TILES + t - 3
                    g = b - 1
                    if isinstance(b, int) and b == 0:
                        return
                if u < XT0:
                    pe.wait_ge(z_lo_ok, NC * g + u - Z0 + 1)
                elif u < W0:
                    pe.wait_ge(xnT_lo_ok, DC * g + u - XT0 + 1)
                elif u < O0:
                    pe.wait_ge(w_lo_ok, DC * g + u - W0 + 1)
                else:
                    pe.wait_ge(y2_ok, NC * g + u - O0 + 1)

            def make_z(b, n, c):
                bank_free(b, Z0 + c)
                if c == 0:
                    pe.wait_ge(xn_lo_ok, b + 1)
                ps = ps_l1[(Z0 + c) % 3][:, 0:D]
                for k in range(NC):
                    a = adj_sb[n][:, k, c * P:(c + 1) * P]
                    nc.tensor.matmul(ps, a, xn_hi[n][:, k, :], start=(k == 0), stop=False)
                    last = nc.tensor.matmul(ps, a, xn_lo[n][:, k, :], start=False, stop=(k == NC - 1))
                last.then_inc(z_ps, 1)

            def transpose_xn(b, n, d):
                bank_free(b, XT0 + d)
                for c in range(NC):
                    last = nc.tensor.transpose(ps_l1[(XT0 + d) % 3][:, c * P:(c + 1) * P],
                                               xn[n][:, c, d * P:(d + 1) * P], ident[:])
                last.then_inc(xnT_ps, 1)

            def make_w(b, n, d):
                bank_free(b, W0 + d)
                ps = ps_l1[(W0 + d) % 3][:, 0:D]
                for k in range(NC):
                    pe.wait_ge(z_lo_ok, NC * b + k + 1)
                    blk = slice(d * P, (d + 1) * P)
                    nc.tensor.matmul(ps, z_hi[:, k, blk], xn_hi[n][:, k, :], start=(k == 0), stop=False)
                    nc.tensor.matmul(ps, z_hi[:, k, blk], xn_lo[n][:, k, :], start=False, stop=False)
                    last = nc.tensor.matmul(ps, z_lo[:, k, blk], xn_hi[n][:, k, :], start=False,
                                            stop=(k == NC - 1))
                last.then_inc(w_ps, 1)

            def make_out(b, c):
                bank_free(b, O0 + c)
                ps = ps_l1[(O0 + c) % 3][:, 0:D]
                blk = slice(c * P, (c + 1) * P)
                for d in range(DC):
                    if c == 0:
                        pe.wait_ge(xnT_lo_ok, DC * b + d + 1)
                        pe.wait_ge(w_lo_ok, DC * b + d + 1)
                    nc.tensor.matmul(ps, xnT_hi[:, d, blk], w_hi[:, d, :], start=(d == 0), stop=False)
                    nc.tensor.matmul(ps, xnT_hi[:, d, blk], w_lo[:, d, :], start=False, stop=False)
                    last = nc.tensor.matmul(ps, xnT_lo[:, d, blk], w_hi[:, d, :], start=False, stop=(d == DC - 1))
                last.then_inc(o_ps, 1)

            bcast_f2(0, 0)

            def step(i, r, n, layer1, prep):
                m, l = (n + 1) % NBUF, (n - 1) % NBUF
                if is_graph(i):
                    transpose_prob(i, 0)
                    transpose_prob(i, 1)
                    attend(i, n, 0)
                    transpose_prob(i, 2)
                    attend(i, n, 1)
                    transpose_prob(i, 3)
                    attend(i, n, 2)
                    attend(i, n, 3)
                if prep:
                    bcast_f2(i + 1, m)
                if layer1:
                    for c in range(NC):
                        make_z(i - 1, l, c)
                    for d in range(DC):
                        transpose_xn(i - 1, l, d)
                    for d in range(DC):
                        make_w(i - 1, l, d)
                    for c in range(NC):
                        make_out(i - 1, c)

            run_steps(pe, step)


def kernel(x, adj, L0_gnn_W_fc, L0_gnn_W_attn):
    import concourse.bacc as bacc
    from concourse.bass_utils import run_bass_kernel_spmd as run

    nc = bacc.Bacc("TRN2", target_bir_lowering=False, num_devices=1)
    arrays = {"x": np.ascontiguousarray(x), "adj": np.ascontiguousarray(adj),
              "w_fc": np.ascontiguousarray(L0_gnn_W_fc), "w_attn": np.ascontiguousarray(L0_gnn_W_attn)}
    ins = [nc.dram_tensor(name, a.shape, mybir.dt.from_np(a.dtype), kind="ExternalInput").ap()
           for name, a in arrays.items()]
    out = nc.dram_tensor("out", x.shape, F32, kind="ExternalOutput").ap()
    program(nc, *ins, out)
    return run(nc, [arrays], core_ids=[0]).results[0]["out"]
```

```python
from contextlib import ExitStack

import numpy as np

import concourse.bass as bass
from concourse import mybir

F32 = mybir.dt.float32
F32R = mybir.dt.float32r
BF16 = mybir.dt.bfloat16
ACT = mybir.ActivationFunctionType
ALU = mybir.AluOpType

P = 128
SLOPE = 0.2
UNIT = 2.0 ** -80
LOWEST = -3e38
LN_EPS = 1e-5
NORM_EPS = 1e-12
NBUF = 3


def program(nc, x, adj, w_fc, w_attn, out):
    B, N, D = x.shape
    O = w_fc.shape[0]
    NC = N // P
    DC = D // P
    HEAD = 3
    LOOPS = (B - 2 - HEAD) // NBUF
    TAIL = HEAD + LOOPS * NBUF

    x_rows = x.rearrange("b (c p) d -> b p c d", p=P)
    adj_rows = adj.rearrange("b (c p) m -> b p c m", p=P)
    out_rows = out.rearrange("b (c p) d -> b p c d", p=P)

    with ExitStack() as ctx:
        def sb(name, shape, dt):
            return ctx.enter_context(nc.sbuf_tensor(name, shape, dt))

        def psum(name):
            return ctx.enter_context(nc.psum_tensor(name, [P, 512], F32))

        def sem(name):
            return ctx.enter_context(nc.semaphore(name))

        ident = sb("ident", [P, P], F32)
        minus_half = sb("minus_half", [P, NC], F32)
        wfc = sb("wfc", [O, D], F32)
        attn_cols = sb("attn_cols", [O, 2], F32)
        attn_wide = sb("attn_wide", [O, 2, P], F32)
        v_bcast = sb("v_bcast", [P, 2, D], F32)
        x_sb = [sb(f"x_sb{n}", [P, NC, D], F32) for n in range(NBUF)]
        x_hi = [sb(f"x_hi{n}", [P, NC, D], F32R) for n in range(NBUF)]
        x_lo = [sb(f"x_lo{n}", [P, NC, D], F32R) for n in range(NBUF)]
        adj_sb = [sb(f"adj_sb{n}", [P, NC, N], F32R) for n in range(NBUF)]
        xn = [sb(f"xn{n}", [P, NC, D], F32) for n in range(NBUF)]
        xn_hi = [sb(f"xn_hi{n}", [P, NC, D], F32R) for n in range(NBUF)]
        xn_lo = [sb(f"xn_lo{n}", [P, NC, D], F32R) for n in range(NBUF)]
        nrm = [sb(f"nrm{n}", [P, NC], F32) for n in range(NBUF)]
        f = [sb(f"f{n}", [P, 2, NC], F32) for n in range(NBUF)]
        scale2 = [sb(f"scale2_{n}", [P, NC], F32) for n in range(NBUF)]
        bias2 = [sb(f"bias2_{n}", [P, NC], F32) for n in range(NBUF)]
        y2 = [sb(f"y2_{n}", [P, NC, D], F32) for n in range(NBUF)]
        neg_max = [sb(f"neg_max{n}", [P, NC], F32) for n in range(NBUF)]
        den = [sb(f"den{n}", [P, NC], F32) for n in range(NBUF)]
        rden = [sb(f"rden{n}", [P, NC], F32) for n in range(NBUF)]
        f2_row = sb("f2_row", [P, N], F32)
        neg_base = sb("neg_base", [P, NC, N], F32)
        score_sb = sb("score_sb", [P, NC, N], F32)
        prob = sb("prob", [P, NC, N], F32)
        probT_hi = sb("probT_hi", [P, NC, N], F32R)
        probT_lo = sb("probT_lo", [P, NC, N], F32R)
        exp_h = sb("exp_h", [P, NC, D], F32)
        relu_h = sb("relu_h", [P, NC, D], F32)
        z_hi = sb("z_hi", [P, NC, D], F32R)
        z_lo = sb("z_lo", [P, NC, D], F32R)
        xnT = sb("xnT", [P, DC, N], F32)
        w_sb = sb("w_sb", [P, DC, D], F32)
        o_sb = sb("o_sb", [P, NC, D], F32)
        product = sb("product", [P, 2, NC, D], BF16)
        row_max = sb("row_max", [P, NC], F32)
        stats = sb("stats", [P, NC, 6], F32)
        mv = sb("mv", [P, NC, 2], F32)
        stats2 = sb("stats2", [P, NC, 6], F32)
        mv2 = sb("mv2", [P, NC, 2], F32)
        ve = sb("ve", [P, NC], F32)
        rstd = sb("rstd", [P, NC], F32)
        rstd_sq = sb("rstd_sq", [P, NC], F32)
        ss = sb("ss", [P, NC], F32)
        ss_floor = sb("ss_floor", [P, NC], F32)
        rnrm = sb("rnrm", [P, NC], F32)
        xn_scale = sb("xn_scale", [P, NC], F32)
        neg_mean = sb("neg_mean", [P, NC], F32)
        xn_bias = sb("xn_bias", [P, NC], F32)
        neg_mean2 = sb("neg_mean2", [P, NC], F32)
        ve2 = sb("ve2", [P, NC], F32)

        ps_f2 = psum("ps_f2")
        ps_probT = [psum(f"ps_probT{n}") for n in range(2)]
        ps_h = [psum(f"ps_h{n}") for n in range(2)]
        ps_l1 = [psum(f"ps_l1_{n}") for n in range(3)]
        Z0, XT0, W0, O0 = 0, NC, NC + DC, NC + 2 * DC
        TILES = 2 * NC + 2 * DC
        assert TILES % 3 == 0

        wfc_in = sem("wfc_in")
        x_in = [sem(f"x_in{n}") for n in range(NBUF)]
        adj_in = [sem(f"adj_in{n}") for n in range(NBUF)]
        out_stored = sem("out_stored")
        consts = sem("consts")
        attn_wide_ok = sem("attn_wide_ok")
        ps_v_ok = sem("ps_v_ok")
        v_ok = sem("v_ok")
        f_ok = sem("f_ok")
        x_hi_ok = sem("x_hi_ok")
        x_lo_ok = sem("x_lo_ok")
        f2_bcast = sem("f2_bcast")
        score_ok = sem("score_ok")
        neg_base_ok = sem("neg_base_ok")
        neg_max_ok = sem("neg_max_ok")
        f2_row_ok = sem("f2_row_ok")
        relu_z_ok = sem("relu_z_ok")
        prob_ok = sem("prob_ok")
        rden_ok = sem("rden_ok")
        probT_ps = sem("probT_ps")
        probT_hi_ok = sem("probT_hi_ok")
        probT_lo_ok = sem("probT_lo_ok")
        h_ps = sem("h_ps")
        elu_ok = sem("elu_ok")
        q_ok = sem("q_ok")
        y_ok = sem("y_ok")
        stats_ok = sem("stats_ok")
        mv_ok = sem("mv_ok")
        norm_step = sem("norm_step")
        norm_ok = sem("norm_ok")
        xn_ok = sem("xn_ok")
        xn_hi_ok = sem("xn_hi_ok")
        xn_lo_ok = sem("xn_lo_ok")
        z_ps = sem("z_ps")
        z_hi_ok = sem("z_hi_ok")
        z_lo_ok = sem("z_lo_ok")
        xnT_ps = sem("xnT_ps")
        xnT_ok = sem("xnT_ok")
        w_ps = sem("w_ps")
        w_ok = sem("w_ok")
        o_ps = sem("o_ps")
        y2_ok = sem("y2_ok")
        stats2_ok = sem("stats2_ok")
        mv2_ok = sem("mv2_ok")
        norm2_step = sem("norm2_step")
        norm2_ok = sem("norm2_ok")
        o_ok = sem("o_ok")

        block = ctx.enter_context(nc.Block())

        def run_steps(eng, step):
            for i in range(HEAD):
                step(i, i // NBUF, i % NBUF, i > 0, True)
            with eng.Fori(0, LOOPS) as j:
                for u in range(NBUF):
                    step(j * NBUF + (HEAD + u), j + (HEAD + u) // NBUF, (HEAD + u) % NBUF, True, True)
            for i in range(TAIL, B):
                step(i, i // NBUF, i % NBUF, True, i + 1 < B)
            for i in range(B, B + 2):
                step(i, i // NBUF, i % NBUF, i == B, False)

        def is_graph(i):
            return not isinstance(i, int) or 0 <= i < B

        @block.sync
        def _(sp):
            def load_x(i, n):
                sp.dma_start(x_sb[n][:], x_rows[i]).then_inc(x_in[n], 16)

            sp.dma_start(wfc[:], w_fc).then_inc(wfc_in, 16)
            for k in range(2):
                sp.dma_start(attn_cols[:, k:k + 1], w_attn[0, k * O:(k + 1) * O].rearrange("(o u) -> o u", u=1),
                             ).then_inc(wfc_in, 16)
            load_x(0, 0)
            load_x(1, 1)

            def step(i, r, n, layer1, prep):
                if (i + 2 < B) if isinstance(i, int) else True:
                    if layer1:
                        sp.wait_ge(y_ok, i)
                    load_x(i + 2, (n + 2) % NBUF)
                if is_graph(i - 2):
                    sp.wait_ge(o_ok, i - 1)
                    sp.dma_start(out_rows[i - 2], o_sb[:]).then_inc(out_stored, 16)

            run_steps(sp, step)
            sp.wait_ge(out_stored, 16 * B)

        @block.gpsimd
        def _(pool):
            def load_adj(i, n):
                pool.dma_start(adj_sb[n][:], adj_rows[i]).then_inc(adj_in[n], 16)

            load_adj(0, 0)
            load_adj(1, 1)
            pool.memset(ident[:], 0.0).then_inc(consts, 1)
            pool.memset(minus_half[:], -0.5).then_inc(consts, 1)
            pool.wait_ge(consts, 2)
            pool.affine_select(out=ident[:], in_=ident[:], compare_op=ALU.not_equal, fill=1.0, base=0,
                               pattern=[[-1, P]], channel_multiplier=1).then_inc(consts, 1)
            pool.wait_ge(consts, 3)

            def split_x(i, n):
                pool.wait_ge(x_hi_ok, i + 1)
                pool.tensor_tensor(x_lo[n][:], x_sb[n][:], x_hi[n][:].bitcast(F32),
                                   ALU.subtract).then_inc(x_lo_ok, 1)

            def split_xn(i, n):
                pool.wait_ge(xn_hi_ok, i + 1)
                pool.tensor_tensor(xn_lo[n][:], xn[n][:], xn_hi[n][:].bitcast(F32),
                                   ALU.subtract).then_inc(xn_lo_ok, 1)

            def residual(i):
                pool.wait_ge(q_ok, i + 1)
                pool.tensor_tensor(relu_h[:], relu_h[:], exp_h[:], ALU.add).then_inc(y_ok, 1)

            def norms(i, n):
                t = 8 * i
                pool.wait_ge(mv_ok, i + 1)
                pool.nop(nofuse=True)
                pool.tensor_scalar(ve[:], mv[:, :, 1], LN_EPS, 1.0, ALU.add, ALU.mult).then_inc(norm_step, 1)
                pool.tensor_scalar(neg_mean[:], mv[:, :, 0], -1.0, 1.0, ALU.mult, ALU.mult).then_inc(norm_step, 1)
                pool.wait_ge(norm_step, t + 2)
                pool.tensor_tensor(rstd[:], ve[:], minus_half[:], ALU.pow).then_inc(norm_step, 1)
                pool.wait_ge(norm_step, t + 3)
                pool.tensor_tensor(rstd_sq[:], rstd[:], rstd[:], ALU.mult).then_inc(norm_step, 1)
                pool.wait_ge(norm_step, t + 4)
                pool.tensor_tensor(ss[:], rstd_sq[:], mv[:, :, 1], ALU.mult).then_inc(norm_step, 1)
                pool.wait_ge(norm_step, t + 5)
                pool.nop(nofuse=True)
                pool.tensor_scalar(ss_floor[:], ss[:], float(D), NORM_EPS, ALU.mult, ALU.max).then_inc(norm_step, 1)
                pool.wait_ge(norm_step, t + 6)
                pool.tensor_tensor(rnrm[:], ss_floor[:], minus_half[:], ALU.pow).then_inc(norm_step, 1)
                pool.wait_ge(norm_step, t + 7)
                if is_graph(i - 1):
                    pool.wait_ge(xn_ok, i)
                pool.tensor_tensor(xn_scale[:], rstd[:], rnrm[:], ALU.mult).then_inc(norm_step, 1)
                pool.tensor_tensor(nrm[n][:], ss_floor[:], rnrm[:], ALU.mult)
                pool.wait_ge(norm_step, t + 8)
                pool.tensor_tensor(xn_bias[:], xn_scale[:], neg_mean[:], ALU.mult).then_inc(norm_ok, 1)

            def norms2(b, n):
                t = 3 * b
                pool.wait_ge(mv2_ok, b + 1)
                pool.nop(nofuse=True)
                pool.tensor_scalar(ve2[:], mv2[:, :, 1], LN_EPS, 1.0, ALU.add, ALU.mult).then_inc(norm2_step, 1)
                pool.tensor_scalar(neg_mean2[:], mv2[:, :, 0], -1.0, 1.0, ALU.mult, ALU.mult).then_inc(norm2_step, 1)
                pool.wait_ge(norm2_step, t + 2)
                pool.tensor_tensor(scale2[n][:], ve2[:], minus_half[:], ALU.pow).then_inc(norm2_step, 1)
                pool.wait_ge(norm2_step, t + 3)
                pool.tensor_tensor(bias2[n][:], scale2[n][:], neg_mean2[:], ALU.mult).then_inc(norm2_ok, 1)

            split_x(0, 0)

            def step(i, r, n, layer1, prep):
                l = (n - 1) % NBUF
                if is_graph(i - 1):
                    split_xn(i - 1, l)
                if prep:
                    split_x(i + 1, (n + 1) % NBUF)
                if is_graph(i):
                    residual(i)
                if (i + 2 < B) if isinstance(i, int) else True:
                    if layer1:
                        pool.wait_ge(z_ps, NC * i)
                    load_adj(i + 2, (n + 2) % NBUF)
                if is_graph(i):
                    norms(i, n)
                if layer1:
                    norms2(i - 1, l)

            run_steps(pool, step)

        @block.vector
        def _(dve):
            dve.wait_ge(wfc_in, 48)
            for k in range(2):
                last = nc.vector.tensor_copy(attn_wide[:, k, :], attn_cols[:, k:k + 1].to_broadcast([O, P]))
            last.then_inc(attn_wide_ok, 1)
            dve.wait_ge(ps_v_ok, 1)
            nc.vector.tensor_scalar(v_bcast[:, 0, :], ps_f2[:, 0:D], (1.0 - SLOPE) * UNIT, None,
                                    ALU.mult).then_inc(v_ok, 1)
            nc.vector.tensor_scalar(v_bcast[:, 1, :], ps_f2[:, D:2 * D], SLOPE * UNIT, None,
                                    ALU.mult).then_inc(v_ok, 1)
            dve.wait_ge(v_ok, 2)

            def node_scores(i, r, n, half):
                dve.wait_ge(x_in[n], 16 * (r + 1))
                if is_graph(i - 1):
                    dve.wait_ge(f_ok, i)
                for k in [half]:
                    for c in range(NC):
                        last = nc.vector.tensor_tensor_reduce(
                            out=product[:, k, c, :], in0=x_sb[n][:, c, :], in1=v_bcast[:, k, :], scale=1.0,
                            scalar=0.0, op0=ALU.mult, op1=ALU.add, accum_out=f[n][:, k, c:c + 1])
                if half == 1:
                    last.then_inc(f_ok, 1)

            def base(i, r, n, c):
                if c == 0:
                    dve.wait_ge(adj_in[n], 16 * (r + 1))
                    dve.wait_ge(f2_row_ok, i + 1)
                    if is_graph(i - 1):
                        dve.wait_ge(score_ok, NC * i)
                nc.vector.scalar_tensor_tensor(out=neg_base[:, c, :], in0=adj_sb[n][:, c, :].bitcast(F32), scalar=0.0,
                                               in1=f2_row[:], op0=ALU.is_equal,
                                               op1=ALU.subtract).then_inc(neg_base_ok, 1)

            def score(i, n, c):
                dve.wait_ge(relu_z_ok, NC * i + c + 1)
                dve.wait_ge(neg_base_ok, NC * i + c + 1)
                dve.nop(nofuse=True)
                nc.vector.tensor_tensor_reduce(
                    out=score_sb[:, c, :], in0=score_sb[:, c, :], in1=neg_base[:, c, :], scale=1.0, scalar=LOWEST,
                    op0=ALU.subtract, op1=ALU.max, accum_out=row_max[:, c:c + 1]).then_inc(score_ok, 1)

            def negate_max(i, n):
                dve.wait_ge(score_ok, NC * (i + 1))
                nc.vector.tensor_scalar(neg_max[n][:], row_max[:], -1.0 / UNIT, None, ALU.mult).then_inc(neg_max_ok, 1)

            def probT_lo_part(i, c):
                dve.wait_ge(probT_hi_ok, NC * i + c + 1)
                nc.vector.tensor_tensor(probT_lo[:, c, :], ps_probT[c % 2][:], probT_hi[:, c, :].bitcast(F32),
                                        ALU.subtract).then_inc(probT_lo_ok, 1)

            def residual(i, n):
                dve.wait_ge(elu_ok, NC * (i + 1))
                nc.vector.scalar_tensor_tensor(out=exp_h[:], in0=exp_h[:], scalar=1.0, in1=x_sb[n][:],
                                               op0=ALU.min, op1=ALU.add).then_inc(q_ok, 1)

            def row_stats(i, n):
                dve.wait_ge(y_ok, i + 1)
                for c in range(NC):
                    nc.vector.bn_stats(stats[:, c, :], relu_h[:, c, :]).then_inc(stats_ok, 1)
                if is_graph(i - 1):
                    dve.wait_ge(norm_ok, i)
                dve.wait_ge(stats_ok, NC * (i + 1))
                dve.nop(nofuse=True)
                for c in range(NC):
                    last = nc.vector.bn_aggr(mv[:, c, :], stats[:, c, :])
                last.then_inc(mv_ok, 1)

            def normalise(i, n):
                dve.wait_ge(norm_ok, i + 1)
                for c in range(NC):
                    last = nc.vector.tensor_scalar(xn[n][:, c, :], relu_h[:, c, :], xn_scale[:, c:c + 1],
                                                   xn_bias[:, c:c + 1], ALU.mult, ALU.add)
                last.then_inc(xn_ok, 1)

            def z_lo_part(b, n, c):
                dve.wait_ge(z_hi_ok, NC * b + c + 1)
                nc.vector.scalar_tensor_tensor(out=z_lo[:, c, :], in0=ps_l1[(Z0 + c) % 3][:, 0:D],
                                               scalar=nrm[n][:, c:c + 1], in1=z_hi[:, c, :].bitcast(F32),
                                               op0=ALU.mult, op1=ALU.subtract).then_inc(z_lo_ok, 1)

            def residual2(b, n, c):
                dve.wait_ge(o_ps, NC * b + c + 1)
                nc.vector.scalar_tensor_tensor(out=y2[n][:, c, :], in0=xn[n][:, c, :], scalar=nrm[n][:, c:c + 1],
                                               in1=ps_l1[(O0 + c) % 3][:, 0:D],
                                               op0=ALU.mult, op1=ALU.add).then_inc(y2_ok, 1)

            def row_stats2(b, n):
                for c in range(NC):
                    dve.wait_ge(y2_ok, NC * b + c + 1)
                    nc.vector.bn_stats(stats2[:, c, :], y2[n][:, c, :]).then_inc(stats2_ok, 1)
                dve.wait_ge(stats2_ok, NC * (b + 1))
                if is_graph(b - 1):
                    dve.wait_ge(norm2_ok, b)
                dve.nop(nofuse=True)
                for c in range(NC):
                    last = nc.vector.bn_aggr(mv2[:, c, :], stats2[:, c, :])
                last.then_inc(mv2_ok, 1)

            node_scores(0, 0, 0, 0)
            node_scores(0, 0, 0, 1)
            for c in range(NC):
                base(0, 0, 0, c)
            for c in range(NC):
                score(0, 0, c)
            negate_max(0, 0)

            def step(i, r, n, layer1, prep):
                m, l = (n + 1) % NBUF, (n - 1) % NBUF
                rm = r + (n + 1) // NBUF
                if is_graph(i):
                    dve.wait_ge(prob_ok, NC * (i + 1))
                    nc.vector.reciprocal(rden[n][:], den[n][:]).then_inc(rden_ok, 1)
                    probT_lo_part(i, 0)
                if prep:
                    node_scores(i + 1, rm, m, 0)
                if is_graph(i):
                    probT_lo_part(i, 1)
                if is_graph(i - 1):
                    normalise(i - 1, l)
                if is_graph(i):
                    probT_lo_part(i, 2)
                if prep:
                    node_scores(i + 1, rm, m, 1)
                if is_graph(i):
                    probT_lo_part(i, 3)
                if prep:
                    base(i + 1, rm, m, 0)
                    base(i + 1, rm, m, 1)
                if is_graph(i):
                    residual(i, n)
                if prep:
                    base(i + 1, rm, m, 2)
                    base(i + 1, rm, m, 3)
                for c in range(NC):
                    if layer1:
                        z_lo_part(i - 1, l, c)
                    if prep:
                        score(i + 1, m, c)
                if prep:
                    negate_max(i + 1, m)
                if is_graph(i):
                    row_stats(i, n)
                if layer1:
                    for c in range(NC):
                        residual2(i - 1, l, c)
                    row_stats2(i - 1, l)

            run_steps(dve, step)

        @block.scalar
        def _(act):
            def x_hi_part(i, r, n):
                act.wait_ge(x_in[n], 16 * (r + 1))
                nc.scalar.activation(x_hi[n][:], x_sb[n][:], ACT.Copy).then_inc(x_hi_ok, 1)

            def copy_f2(i):
                act.wait_ge(f2_bcast, i + 1)
                if is_graph(i - 1):
                    act.wait_ge(neg_base_ok, NC * i)
                nc.scalar.activation(f2_row[:], ps_f2[:], ACT.Copy).then_inc(f2_row_ok, 1)

            def relu_z(i, n, c):
                if c == 0:
                    act.wait_ge(f2_row_ok, i + 1)
                    if is_graph(i - 1):
                        act.wait_ge(prob_ok, NC * i)
                nc.scalar.activation(score_sb[:, c, :], f2_row[:], ACT.Relu, bias=f[n][:, 0, c:c + 1],
                                     scale=(1.0 - SLOPE) / SLOPE).then_inc(relu_z_ok, 1)

            def softmax_exp(i, n, c):
                if c == 0:
                    act.wait_ge(neg_max_ok, i + 1)
                if not isinstance(i, int) or i > 0:
                    act.wait_ge(probT_ps, NC * (i - 1) + c + 1)
                nc.scalar.activation(prob[:, c, :], score_sb[:, c, :], ACT.Exp, bias=neg_max[n][:, c:c + 1], scale=1.0 / UNIT,
                                     accum_out=den[n][:, c:c + 1]).then_inc(prob_ok, 1)

            def probT_hi_part(i, c):
                act.wait_ge(probT_ps, NC * i + c + 1)
                if not isinstance(i, int) or i > 0:
                    act.wait_ge(h_ps, NC * (i - 1) + c + 1)
                nc.scalar.activation(probT_hi[:, c, :], ps_probT[c % 2][:], ACT.Copy).then_inc(probT_hi_ok, 1)

            def elu_parts(i, n, c):
                if c == 0:
                    act.wait_ge(rden_ok, i + 1)
                    if not isinstance(i, int) or i > 0:
                        act.wait_ge(xn_ok, i)
                act.wait_ge(h_ps, NC * i + c + 1)
                nc.scalar.activation(exp_h[:, c, :], ps_h[c % 2][:, 0:D], ACT.Exp, scale=rden[n][:, c:c + 1])
                nc.scalar.activation(relu_h[:, c, :], ps_h[c % 2][:, 0:D], ACT.Relu,
                                     scale=rden[n][:, c:c + 1]).then_inc(elu_ok, 1)

            def xn_hi_part(i, n):
                act.wait_ge(xn_ok, i + 1)
                nc.scalar.activation(xn_hi[n][:], xn[n][:], ACT.Copy).then_inc(xn_hi_ok, 1)

            def z_hi_part(b, n, c):
                act.wait_ge(z_ps, NC * b + c + 1)
                if c == 0 and (not isinstance(b, int) or b > 0):
                    act.wait_ge(w_ps, DC * b)
                nc.scalar.activation(z_hi[:, c, :], ps_l1[(Z0 + c) % 3][:, 0:D], ACT.Copy,
                                     scale=nrm[n][:, c:c + 1]).then_inc(z_hi_ok, 1)

            def copy_xnT(b, d):
                act.wait_ge(xnT_ps, DC * b + d + 1)
                if d == 0 and is_graph(b - 1):
                    act.wait_ge(o_ps, NC * b)
                nc.scalar.activation(xnT[:, d, :], ps_l1[(XT0 + d) % 3][:], ACT.Copy).then_inc(xnT_ok, 1)

            def copy_w(b, d):
                act.wait_ge(w_ps, DC * b + d + 1)
                nc.scalar.activation(w_sb[:, d, :], ps_l1[(W0 + d) % 3][:, 0:D], ACT.Copy).then_inc(w_ok, 1)

            def normalise2(b, n):
                act.wait_ge(norm2_ok, b + 1)
                if is_graph(b - 1):
                    act.wait_ge(out_stored, 16 * b)
                for c in range(NC):
                    last = nc.scalar.activation(o_sb[:, c, :], y2[n][:, c, :], ACT.Identity,
                                                bias=bias2[n][:, c:c + 1], scale=scale2[n][:, c:c + 1])
                last.then_inc(o_ok, 1)

            x_hi_part(0, 0, 0)
            copy_f2(0)
            for c in range(NC):
                relu_z(0, 0, c)
            for c in range(NC):
                softmax_exp(0, 0, c)

            def step(i, r, n, layer1, prep):
                m, l = (n + 1) % NBUF, (n - 1) % NBUF
                if is_graph(i):
                    probT_hi_part(i, 0)
                if prep:
                    x_hi_part(i + 1, r + (n + 1) // NBUF, m)
                if is_graph(i):
                    probT_hi_part(i, 1)
                    probT_hi_part(i, 2)
                if is_graph(i - 1):
                    xn_hi_part(i - 1, l)
                if is_graph(i):
                    elu_parts(i, n, 0)
                    probT_hi_part(i, 3)
                    elu_parts(i, n, 1)
                    elu_parts(i, n, 2)
                    elu_parts(i, n, 3)
                if prep:
                    copy_f2(i + 1)
                for c in range(NC):
                    if prep:
                        relu_z(i + 1, m, c)
                    if layer1:
                        z_hi_part(i - 1, l, c)
                if is_graph(i - 2):
                    normalise2(i - 2, (n - 2) % NBUF)
                if layer1:
                    for d in range(DC):
                        copy_xnT(i - 1, d)
                if prep:
                    softmax_exp(i + 1, m, 0)
                    softmax_exp(i + 1, m, 1)
                if layer1:
                    copy_w(i - 1, 0)
                if prep:
                    softmax_exp(i + 1, m, 2)
                if layer1:
                    copy_w(i - 1, 1)
                if prep:
                    softmax_exp(i + 1, m, 3)

            run_steps(act, step)

        @block.tensor
        def _(pe):
            pe.wait_ge(attn_wide_ok, 1)
            for k in range(2):
                last = nc.tensor.matmul(ps_f2[:, k * D:(k + 1) * D], attn_wide[:, k, :], wfc[:], start=True, stop=True)
            last.then_inc(ps_v_ok, 1)

            def bcast_f2(i, n):
                pe.wait_ge(f_ok, i + 1)
                if isinstance(i, int) and i == 0:
                    pe.wait_ge(v_ok, 2)
                    pe.wait_ge(consts, 3)
                else:
                    pe.wait_ge(f2_row_ok, i)
                for c in range(NC):
                    last = nc.tensor.transpose(ps_f2[:, c * P:(c + 1) * P],
                                               f[n][:, 1, c:c + 1].to_broadcast([P, P]), ident[:])
                last.then_inc(f2_bcast, 1)

            def transpose_prob(i, c):
                pe.wait_ge(prob_ok, NC * i + c + 1)
                if c >= 2:
                    pe.wait_ge(probT_lo_ok, NC * i + c - 1)
                elif not isinstance(i, int) or i > 0:
                    pe.wait_ge(probT_lo_ok, NC * i + c - 1)
                for k in range(NC):
                    last = nc.tensor.transpose(ps_probT[c % 2][:, k * P:(k + 1) * P],
                                               prob[:, c, k * P:(k + 1) * P], ident[:])
                last.then_inc(probT_ps, 1)

            def attend(i, n, c):
                pe.wait_ge(probT_lo_ok, NC * i + c + 1)
                if c == 0:
                    pe.wait_ge(x_lo_ok, i + 1)
                if c >= 2 or not isinstance(i, int) or i > 0:
                    pe.wait_ge(elu_ok, NC * i + c - 1)
                for k in range(NC):
                    blk = slice(k * P, (k + 1) * P)
                    ps = ps_h[c % 2][:, 0:D]
                    nc.tensor.matmul(ps, probT_hi[:, c, blk], x_hi[n][:, k, :], start=(k == 0), stop=False)
                    nc.tensor.matmul(ps, probT_hi[:, c, blk], x_lo[n][:, k, :], start=False, stop=False)
                    last = nc.tensor.matmul(ps, probT_lo[:, c, blk], x_hi[n][:, k, :], start=False,
                                            stop=(k == NC - 1))
                last.then_inc(h_ps, 1)

            def bank_free(b, t):
                if t >= 3:
                    u = t - 3
                    g = b
                else:
                    u = TILES + t - 3
                    g = b - 1
                    if isinstance(b, int) and b == 0:
                        return
                if u < XT0:
                    pe.wait_ge(z_lo_ok, NC * g + u - Z0 + 1)
                elif u < W0:
                    pe.wait_ge(xnT_ok, DC * g + u - XT0 + 1)
                elif u < O0:
                    pe.wait_ge(w_ok, DC * g + u - W0 + 1)
                else:
                    pe.wait_ge(y2_ok, NC * g + u - O0 + 1)

            def make_z(b, n, c):
                bank_free(b, Z0 + c)
                if c == 0:
                    pe.wait_ge(xn_lo_ok, b + 1)
                ps = ps_l1[(Z0 + c) % 3][:, 0:D]
                for k in range(NC):
                    a = adj_sb[n][:, k, c * P:(c + 1) * P]
                    nc.tensor.matmul(ps, a, xn_hi[n][:, k, :], start=(k == 0), stop=False)
                    last = nc.tensor.matmul(ps, a, xn_lo[n][:, k, :], start=False, stop=(k == NC - 1))
                last.then_inc(z_ps, 1)

            def transpose_xn(b, n, d):
                bank_free(b, XT0 + d)
                for c in range(NC):
                    last = nc.tensor.transpose(ps_l1[(XT0 + d) % 3][:, c * P:(c + 1) * P],
                                               xn[n][:, c, d * P:(d + 1) * P], ident[:])
                last.then_inc(xnT_ps, 1)

            def make_w(b, n, d):
                bank_free(b, W0 + d)
                ps = ps_l1[(W0 + d) % 3][:, 0:D]
                for k in range(NC):
                    pe.wait_ge(z_lo_ok, NC * b + k + 1)
                    blk = slice(d * P, (d + 1) * P)
                    nc.tensor.matmul(ps, z_hi[:, k, blk], xn_hi[n][:, k, :], start=(k == 0), stop=False)
                    nc.tensor.matmul(ps, z_hi[:, k, blk], xn_lo[n][:, k, :], start=False, stop=False)
                    last = nc.tensor.matmul(ps, z_lo[:, k, blk], xn_hi[n][:, k, :], start=False,
                                            stop=(k == NC - 1))
                last.then_inc(w_ps, 1)

            def make_out(b, c):
                bank_free(b, O0 + c)
                ps = ps_l1[(O0 + c) % 3][:, 0:D]
                for d in range(DC):
                    if c == 0:
                        pe.wait_ge(xnT_ok, DC * b + d + 1)
                        pe.wait_ge(w_ok, DC * b + d + 1)
                    last = nc.tensor.matmul(ps, xnT[:, d, c * P:(c + 1) * P], w_sb[:, d, :], start=(d == 0),
                                            stop=(d == DC - 1))
                last.then_inc(o_ps, 1)

            bcast_f2(0, 0)

            def step(i, r, n, layer1, prep):
                m, l = (n + 1) % NBUF, (n - 1) % NBUF
                if is_graph(i):
                    transpose_prob(i, 0)
                    transpose_prob(i, 1)
                    attend(i, n, 0)
                    transpose_prob(i, 2)
                    attend(i, n, 1)
                    transpose_prob(i, 3)
                    attend(i, n, 2)
                    attend(i, n, 3)
                if prep:
                    bcast_f2(i + 1, m)
                if layer1:
                    for c in range(NC):
                        make_z(i - 1, l, c)
                    for d in range(DC):
                        transpose_xn(i - 1, l, d)
                    for d in range(DC):
                        make_w(i - 1, l, d)
                    for c in range(NC):
                        make_out(i - 1, c)

            run_steps(pe, step)


def kernel(x, adj, L0_gnn_W_fc, L0_gnn_W_attn):
    import concourse.bacc as bacc
    from concourse.bass_utils import run_bass_kernel_spmd as run

    nc = bacc.Bacc("TRN2", target_bir_lowering=False, num_devices=1)
    arrays = {"x": np.ascontiguousarray(x), "adj": np.ascontiguousarray(adj),
              "w_fc": np.ascontiguousarray(L0_gnn_W_fc), "w_attn": np.ascontiguousarray(L0_gnn_W_attn)}
    ins = [nc.dram_tensor(name, a.shape, mybir.dt.from_np(a.dtype), kind="ExternalInput").ap()
           for name, a in arrays.items()]
    out = nc.dram_tensor("out", x.shape, F32, kind="ExternalOutput").ap()
    program(nc, *ins, out)
    return run(nc, [arrays], core_ids=[0]).results[0]["out"]
```

```python
from contextlib import ExitStack

import numpy as np

import concourse.bass as bass
from concourse import mybir

F32 = mybir.dt.float32
F32R = mybir.dt.float32r
BF16 = mybir.dt.bfloat16
ACT = mybir.ActivationFunctionType
ALU = mybir.AluOpType

P = 128
SLOPE = 0.2
UNIT = 2.0 ** -80
LOWEST = -3e38
LN_EPS = 1e-5
NORM_EPS = 1e-12
NBUF = 3


def program(nc, x, adj, w_fc, w_attn, out):
    B, N, D = x.shape
    O = w_fc.shape[0]
    NC = N // P
    DC = D // P
    HEAD = 3
    LOOPS = (B - 2 - HEAD) // NBUF
    TAIL = HEAD + LOOPS * NBUF

    x_rows = x.rearrange("b (c p) d -> b p c d", p=P)
    adj_rows = adj.rearrange("b (c p) m -> b p c m", p=P)
    out_rows = out.rearrange("b (c p) d -> b p c d", p=P)

    with ExitStack() as ctx:
        def sb(name, shape, dt):
            return ctx.enter_context(nc.sbuf_tensor(name, shape, dt))

        def psum(name):
            return ctx.enter_context(nc.psum_tensor(name, [P, 512], F32))

        def sem(name):
            return ctx.enter_context(nc.semaphore(name))

        ident = sb("ident", [P, P], F32)
        minus_half = sb("minus_half", [P, NC], F32)
        wfc = sb("wfc", [O, D], F32)
        attn_cols = sb("attn_cols", [O, 2], F32)
        attn_wide = sb("attn_wide", [O, 2, P], F32)
        v_bcast = sb("v_bcast", [P, 2, D], F32)
        x_sb = [sb(f"x_sb{n}", [P, NC, D], F32) for n in range(NBUF)]
        x_hi = [sb(f"x_hi{n}", [P, NC, D], F32R) for n in range(NBUF)]
        x_lo = [sb(f"x_lo{n}", [P, NC, D], F32R) for n in range(NBUF)]
        adj_sb = [sb(f"adj_sb{n}", [P, NC, N], F32R) for n in range(NBUF)]
        xn = [sb(f"xn{n}", [P, NC, D], F32) for n in range(NBUF)]
        xn_hi = [sb(f"xn_hi{n}", [P, NC, D], F32R) for n in range(NBUF)]
        xn_lo = [sb(f"xn_lo{n}", [P, NC, D], F32R) for n in range(NBUF)]
        nrm = [sb(f"nrm{n}", [P, NC], F32) for n in range(NBUF)]
        f = [sb(f"f{n}", [P, 2, NC], F32) for n in range(NBUF)]
        y = [sb(f"y{n}", [P, NC, D], F32) for n in range(NBUF)]
        scale2 = [sb(f"scale2_{n}", [P, NC], F32) for n in range(NBUF)]
        bias2 = [sb(f"bias2_{n}", [P, NC], F32) for n in range(NBUF)]
        y2 = [sb(f"y2_{n}", [P, NC, D], F32) for n in range(NBUF)]
        neg_max = [sb(f"neg_max{n}", [P, NC], F32) for n in range(NBUF)]
        den = [sb(f"den{n}", [P, NC], F32) for n in range(NBUF)]
        rden = [sb(f"rden{n}", [P, NC], F32) for n in range(NBUF)]
        f2_row = sb("f2_row", [P, N], F32)
        neg_base = sb("neg_base", [P, NC, N], F32)
        score_sb = sb("score_sb", [P, NC, N], F32)
        prob = sb("prob", [P, NC, N], F32)
        probT_hi = sb("probT_hi", [P, NC, N], F32R)
        probT_lo = sb("probT_lo", [P, NC, N], F32R)
        exp_h = sb("exp_h", [P, NC, D], F32)
        z_sb = sb("z_sb", [P, NC, D], F32)
        xnT = sb("xnT", [P, DC, N], F32)
        w_sb = sb("w_sb", [P, DC, D], F32)
        o_sb = sb("o_sb", [P, NC, D], F32)
        product = sb("product", [P, 2, NC, D], BF16)
        row_max = sb("row_max", [P, NC], F32)
        stats = sb("stats", [P, NC, 6], F32)
        mv = sb("mv", [P, NC, 2], F32)
        stats2 = sb("stats2", [P, NC, 6], F32)
        mv2 = sb("mv2", [P, NC, 2], F32)
        ve = sb("ve", [P, NC], F32)
        rstd = sb("rstd", [P, NC], F32)
        rstd_sq = sb("rstd_sq", [P, NC], F32)
        ss = sb("ss", [P, NC], F32)
        ss_floor = sb("ss_floor", [P, NC], F32)
        rnrm = sb("rnrm", [P, NC], F32)
        xn_scale = sb("xn_scale", [P, NC], F32)
        neg_mean = sb("neg_mean", [P, NC], F32)
        xn_bias = sb("xn_bias", [P, NC], F32)
        neg_mean2 = sb("neg_mean2", [P, NC], F32)
        ve2 = sb("ve2", [P, NC], F32)

        ps_f2 = psum("ps_f2")
        ps_probT = [psum(f"ps_probT{n}") for n in range(2)]
        ps_h = [psum(f"ps_h{n}") for n in range(2)]
        ps_l1 = [psum(f"ps_l1_{n}") for n in range(3)]
        Z0, XT0, W0, O0 = 0, NC, NC + DC, NC + 2 * DC
        TILES = 2 * NC + 2 * DC
        assert TILES % 3 == 0

        wfc_in = sem("wfc_in")
        x_in = [sem(f"x_in{n}") for n in range(NBUF)]
        adj_in = [sem(f"adj_in{n}") for n in range(NBUF)]
        out_stored = sem("out_stored")
        consts = sem("consts")
        attn_wide_ok = sem("attn_wide_ok")
        ps_v_ok = sem("ps_v_ok")
        v_ok = sem("v_ok")
        f_ok = sem("f_ok")
        x_hi_ok = sem("x_hi_ok")
        x_lo_ok = sem("x_lo_ok")
        f2_bcast = sem("f2_bcast")
        score_ok = sem("score_ok")
        neg_base_ok = sem("neg_base_ok")
        neg_max_ok = sem("neg_max_ok")
        f2_row_ok = sem("f2_row_ok")
        relu_z_ok = sem("relu_z_ok")
        prob_ok = sem("prob_ok")
        rden_ok = sem("rden_ok")
        probT_ps = sem("probT_ps")
        probT_hi_ok = sem("probT_hi_ok")
        probT_lo_ok = sem("probT_lo_ok")
        h_ps = sem("h_ps")
        elu_ok = sem("elu_ok")
        q_ok = sem("q_ok")
        y_ok = sem("y_ok")
        stats_ok = sem("stats_ok")
        mv_ok = sem("mv_ok")
        norm_step = sem("norm_step")
        norm_ok = sem("norm_ok")
        xn_ok = sem("xn_ok")
        xn_hi_ok = sem("xn_hi_ok")
        xn_lo_ok = sem("xn_lo_ok")
        z_ps = sem("z_ps")
        z_ok = sem("z_ok")
        xnT_ps = sem("xnT_ps")
        xnT_ok = sem("xnT_ok")
        w_ps = sem("w_ps")
        w_ok = sem("w_ok")
        o_ps = sem("o_ps")
        y2_ok = sem("y2_ok")
        stats2_ok = sem("stats2_ok")
        mv2_ok = sem("mv2_ok")
        norm2_step = sem("norm2_step")
        norm2_ok = sem("norm2_ok")
        o_ok = sem("o_ok")
        y_edge = sem("y_edge")
        xn_lo_last = sem("xn_lo_last")
        q_last = sem("q_last")
        o_last = sem("o_last")
        half_stored = sem("half_stored")

        block = ctx.enter_context(nc.Block())

        def run_steps(eng, step):
            for i in range(HEAD):
                step(i, i // NBUF, i % NBUF, i > 0, True)
            with eng.Fori(0, LOOPS) as j:
                for u in range(NBUF):
                    step(j * NBUF + (HEAD + u), j + (HEAD + u) // NBUF, (HEAD + u) % NBUF, True, True)
            for i in range(TAIL, B):
                step(i, i // NBUF, i % NBUF, True, i + 1 < B)
            for i in range(B, B + 2):
                step(i, i // NBUF, i % NBUF, i == B, False)

        def is_graph(i):
            return not isinstance(i, int) or 0 <= i < B

        def edge(i):
            return {0: 1, B - 1: 2}.get(i, 0) if isinstance(i, int) else 0

        def wait_y(eng, i):
            if edge(i):
                eng.wait_ge(y_edge, edge(i))
            else:
                eng.wait_ge(y_ok, i)

        @block.sync
        def _(sp):
            def load_x(i, n):
                sp.dma_start(x_sb[n][:], x_rows[i]).then_inc(x_in[n], 16)

            for k in range(2):
                sp.dma_start(attn_cols[:, k:k + 1], w_attn[0, k * O:(k + 1) * O].rearrange("(o u) -> o u", u=1),
                             ).then_inc(wfc_in, 16)
            sp.dma_start(wfc[:], w_fc).then_inc(wfc_in, 16)
            load_x(0, 0)
            load_x(1, 1)

            def step(i, r, n, layer1, prep):
                if is_graph(i + 2):
                    if layer1:
                        wait_y(sp, i - 1)
                    load_x(i + 2, (n + 2) % NBUF)
                if is_graph(i - 2) and (not isinstance(i, int) or i < B + 1):
                    sp.wait_ge(o_ok, i - 1)
                    sp.dma_start(out_rows[i - 2], o_sb[:]).then_inc(out_stored, 16)

            run_steps(sp, step)
            h = NC // 2
            sp.wait_ge(o_last, 1)
            sp.dma_start(out_rows[B - 1][:, h:NC], o_sb[:, h:NC]).then_inc(half_stored, 16)
            sp.wait_ge(o_ok, B)
            sp.dma_start(out_rows[B - 1][:, 0:h], o_sb[:, 0:h]).then_inc(out_stored, 16)
            sp.wait_ge(half_stored, 16)
            sp.wait_ge(out_stored, 16 * B)

        @block.gpsimd
        def _(pool):
            def load_adj(i, n):
                pool.dma_start(adj_sb[n][:], adj_rows[i]).then_inc(adj_in[n], 16)

            pool.memset(ident[:], 0.0).then_inc(consts, 1)
            pool.memset(minus_half[:], -0.5).then_inc(consts, 1)
            pool.wait_ge(consts, 2)
            pool.affine_select(out=ident[:], in_=ident[:], compare_op=ALU.not_equal, fill=1.0, base=0,
                               pattern=[[-1, P]], channel_multiplier=1).then_inc(consts, 1)
            pool.wait_ge(wfc_in, 48)
            load_adj(0, 0)
            load_adj(1, 1)

            def split_x(i, n):
                pool.wait_ge(x_hi_ok, i + 1)
                pool.tensor_tensor(x_lo[n][:], x_sb[n][:], x_hi[n][:].bitcast(F32),
                                   ALU.subtract).then_inc(x_lo_ok, 1)

            def split_xn(i, n):
                pool.wait_ge(xn_hi_ok, i + 1)
                pool.tensor_tensor(xn_lo[n][:], xn[n][:], xn_hi[n][:].bitcast(F32),
                                   ALU.subtract).then_inc(xn_lo_ok, 1)

            def residual(i, n):
                pool.wait_ge(q_ok, i + 1)
                pool.tensor_tensor(y[n][:], y[n][:], exp_h[:], ALU.add).then_inc(y_ok, 1)

            def norms(i, n):
                t = 8 * i
                pool.wait_ge(mv_ok, i + 1)
                pool.nop(nofuse=True)
                pool.tensor_scalar(ve[:], mv[:, :, 1], LN_EPS, 1.0, ALU.add, ALU.mult).then_inc(norm_step, 1)
                pool.tensor_scalar(neg_mean[:], mv[:, :, 0], -1.0, 1.0, ALU.mult, ALU.mult).then_inc(norm_step, 1)
                pool.wait_ge(norm_step, t + 2)
                pool.tensor_tensor(rstd[:], ve[:], minus_half[:], ALU.pow).then_inc(norm_step, 1)
                pool.wait_ge(norm_step, t + 3)
                pool.tensor_tensor(rstd_sq[:], rstd[:], rstd[:], ALU.mult).then_inc(norm_step, 1)
                pool.wait_ge(norm_step, t + 4)
                pool.tensor_tensor(ss[:], rstd_sq[:], mv[:, :, 1], ALU.mult).then_inc(norm_step, 1)
                pool.wait_ge(norm_step, t + 5)
                pool.nop(nofuse=True)
                pool.tensor_scalar(ss_floor[:], ss[:], float(D), NORM_EPS, ALU.mult, ALU.max).then_inc(norm_step, 1)
                pool.wait_ge(norm_step, t + 6)
                pool.tensor_tensor(rnrm[:], ss_floor[:], minus_half[:], ALU.pow).then_inc(norm_step, 1)
                pool.wait_ge(norm_step, t + 7)
                if is_graph(i - 1):
                    pool.wait_ge(xn_ok, i)
                pool.tensor_tensor(xn_scale[:], rstd[:], rnrm[:], ALU.mult).then_inc(norm_step, 1)
                pool.tensor_tensor(nrm[n][:], ss_floor[:], rnrm[:], ALU.mult)
                pool.wait_ge(norm_step, t + 8)
                pool.tensor_tensor(xn_bias[:], xn_scale[:], neg_mean[:], ALU.mult).then_inc(norm_ok, 1)

            def norms2(b, n):
                t = 3 * b
                pool.wait_ge(mv2_ok, b + 1)
                pool.nop(nofuse=True)
                pool.tensor_scalar(ve2[:], mv2[:, :, 1], LN_EPS, 1.0, ALU.add, ALU.mult).then_inc(norm2_step, 1)
                pool.tensor_scalar(neg_mean2[:], mv2[:, :, 0], -1.0, 1.0, ALU.mult, ALU.mult).then_inc(norm2_step, 1)
                pool.wait_ge(norm2_step, t + 2)
                pool.tensor_tensor(scale2[n][:], ve2[:], minus_half[:], ALU.pow).then_inc(norm2_step, 1)
                pool.wait_ge(norm2_step, t + 3)
                pool.tensor_tensor(bias2[n][:], scale2[n][:], neg_mean2[:], ALU.mult).then_inc(norm2_ok, 1)

            split_x(0, 0)

            def step(i, r, n, layer1, prep):
                if is_graph(i - 1) and edge(i - 1) != 2:
                    split_xn(i - 1, (n - 1) % NBUF)
                if is_graph(i - 2):
                    norms2(i - 2, (n - 2) % NBUF)
                if prep and not layer1:
                    split_x(i + 1, (n + 1) % NBUF)
                if is_graph(i) and not edge(i):
                    residual(i, n)
                if prep and layer1:
                    split_x(i + 1, (n + 1) % NBUF)
                if is_graph(i + 2):
                    if layer1:
                        pool.wait_ge(z_ps, NC * i)
                    load_adj(i + 2, (n + 2) % NBUF)
                if is_graph(i):
                    norms(i, n)

            run_steps(pool, step)

        @block.vector
        def _(dve):
            dve.wait_ge(wfc_in, 48)
            for k in range(2):
                last = nc.vector.tensor_copy(attn_wide[:, k, :], attn_cols[:, k:k + 1].to_broadcast([O, P]))
            last.then_inc(attn_wide_ok, 1)
            dve.wait_ge(ps_v_ok, 1)
            nc.vector.tensor_scalar(v_bcast[:, 0, :], ps_f2[:, 0:D], (1.0 - SLOPE) * UNIT, None,
                                    ALU.mult).then_inc(v_ok, 1)
            nc.vector.tensor_scalar(v_bcast[:, 1, :], ps_f2[:, D:2 * D], SLOPE * UNIT, None,
                                    ALU.mult).then_inc(v_ok, 1)
            dve.wait_ge(v_ok, 2)

            def node_scores(i, r, n, k):
                dve.wait_ge(x_in[n], 16 * (r + 1))
                if is_graph(i - 1):
                    dve.wait_ge(f_ok, 2 * i)
                for c in range(NC):
                    last = nc.vector.tensor_tensor_reduce(
                        out=product[:, k, c, :], in0=x_sb[n][:, c, :], in1=v_bcast[:, k, :], scale=1.0,
                        scalar=0.0, op0=ALU.mult, op1=ALU.add, accum_out=f[n][:, k, c:c + 1])
                last.then_inc(f_ok, 1)

            def base(i, r, n, c):
                if c == 0:
                    dve.wait_ge(adj_in[n], 16 * (r + 1))
                    dve.wait_ge(f2_row_ok, i + 1)
                    if is_graph(i - 1):
                        dve.wait_ge(score_ok, NC * i)
                nc.vector.scalar_tensor_tensor(out=neg_base[:, c, :], in0=adj_sb[n][:, c, :].bitcast(F32), scalar=0.0,
                                               in1=f2_row[:], op0=ALU.is_equal,
                                               op1=ALU.subtract).then_inc(neg_base_ok, 1)

            def score(i, n, c):
                dve.wait_ge(relu_z_ok, NC * i + c + 1)
                dve.wait_ge(neg_base_ok, NC * i + c + 1)
                dve.nop(nofuse=True)
                nc.vector.tensor_tensor_reduce(
                    out=score_sb[:, c, :], in0=score_sb[:, c, :], in1=neg_base[:, c, :], scale=1.0, scalar=LOWEST,
                    op0=ALU.subtract, op1=ALU.max, accum_out=row_max[:, c:c + 1]).then_inc(score_ok, 1)

            def negate_max(i, n, c):
                dve.wait_ge(score_ok, NC * i + c + 1)
                nc.vector.tensor_scalar(neg_max[n][:, c:c + 1], row_max[:, c:c + 1], -1.0 / UNIT, None,
                                        ALU.mult).then_inc(neg_max_ok, 1)

            def denominators(i, n):
                dve.wait_ge(prob_ok, NC * (i + 1))
                nc.vector.reciprocal(rden[n][:], den[n][:]).then_inc(rden_ok, 1)

            def probT_lo_part(i, c):
                dve.wait_ge(probT_hi_ok, NC * i + c + 1)
                nc.vector.tensor_tensor(probT_lo[:, c, :], ps_probT[c % 2][:], probT_hi[:, c, :].bitcast(F32),
                                        ALU.subtract).then_inc(probT_lo_ok, 1)

            def residual(i, n):
                dve.wait_ge(elu_ok, NC * (i + 1))
                nc.vector.scalar_tensor_tensor(out=exp_h[:], in0=exp_h[:], scalar=1.0, in1=x_sb[n][:],
                                               op0=ALU.min, op1=ALU.add).then_inc(q_ok, 1)

            def last_residual(i, n):
                for c in range(NC):
                    dve.wait_ge(elu_ok, NC * i + c + 1)
                    nc.vector.scalar_tensor_tensor(out=exp_h[:, c, :], in0=exp_h[:, c, :], scalar=1.0,
                                                   in1=x_sb[n][:, c, :], op0=ALU.min, op1=ALU.add).then_inc(q_last, 1)
                    dve.wait_ge(q_last, c + 1)
                    last = nc.vector.tensor_tensor(y[n][:, c, :], y[n][:, c, :], exp_h[:, c, :], ALU.add)
                last.then_inc(y_edge, 1)

            def split_last_xn(i, n):
                dve.wait_ge(xn_hi_ok, i + 1)
                nc.vector.tensor_tensor(xn_lo[n][:], xn[n][:], xn_hi[n][:].bitcast(F32),
                                        ALU.subtract).then_inc(xn_lo_last, 1)

            def row_stats(i, n):
                wait_y(dve, i)
                for c in range(NC):
                    nc.vector.bn_stats(stats[:, c, :], y[n][:, c, :]).then_inc(stats_ok, 1)
                if is_graph(i - 1):
                    dve.wait_ge(norm_ok, i)
                dve.wait_ge(stats_ok, NC * (i + 1))
                dve.nop(nofuse=True)
                for c in range(NC):
                    last = nc.vector.bn_aggr(mv[:, c, :], stats[:, c, :])
                last.then_inc(mv_ok, 1)

            def normalise(i, n):
                dve.wait_ge(norm_ok, i + 1)
                for c in range(NC):
                    last = nc.vector.tensor_scalar(xn[n][:, c, :], y[n][:, c, :], xn_scale[:, c:c + 1],
                                                   xn_bias[:, c:c + 1], ALU.mult, ALU.add)
                last.then_inc(xn_ok, 1)

            def residual2(b, n, c):
                dve.wait_ge(o_ps, NC * b + c + 1)
                nc.vector.scalar_tensor_tensor(out=y2[n][:, c, :], in0=xn[n][:, c, :], scalar=nrm[n][:, c:c + 1],
                                               in1=ps_l1[(O0 + c) % 3][:, 0:D],
                                               op0=ALU.mult, op1=ALU.add).then_inc(y2_ok, 1)
                if edge(b) == 2:
                    dve.wait_ge(y2_ok, NC * b + c + 1)
                    nc.vector.bn_stats(stats2[:, c, :], y2[n][:, c, :]).then_inc(stats2_ok, 1)

            def row_stats2(b, n):
                for c in range(NC):
                    dve.wait_ge(y2_ok, NC * b + c + 1)
                    nc.vector.bn_stats(stats2[:, c, :], y2[n][:, c, :]).then_inc(stats2_ok, 1)
                dve.wait_ge(stats2_ok, NC * (b + 1))
                if is_graph(b - 1):
                    dve.wait_ge(norm2_ok, b)
                dve.nop(nofuse=True)
                for c in range(NC):
                    last = nc.vector.bn_aggr(mv2[:, c, :], stats2[:, c, :])
                last.then_inc(mv2_ok, 1)

            def row_stats2_end(b, n):
                dve.wait_ge(stats2_ok, NC * (b + 1))
                dve.wait_ge(norm2_ok, b)
                dve.nop(nofuse=True)
                for c in range(NC):
                    last = nc.vector.bn_aggr(mv2[:, c, :], stats2[:, c, :])
                last.then_inc(mv2_ok, 1)

            def normalise2_half(b, n):
                dve.wait_ge(norm2_ok, b + 1)
                dve.wait_ge(out_stored, 16 * b)
                for c in range(NC // 2, NC):
                    last = nc.vector.tensor_scalar(o_sb[:, c, :], y2[n][:, c, :], scale2[n][:, c:c + 1],
                                                   bias2[n][:, c:c + 1], ALU.mult, ALU.add)
                last.then_inc(o_last, 1)

            node_scores(0, 0, 0, 1)
            node_scores(0, 0, 0, 0)
            node_scores(1, 0, 1, 1)
            base(0, 0, 0, 0)
            for c in range(NC):
                if c + 1 < NC:
                    base(0, 0, 0, c + 1)
                score(0, 0, c)
                negate_max(0, 0, c)
                if c >= 2:
                    probT_lo_part(0, c - 2)
            denominators(0, 0)
            node_scores(1, 0, 1, 0)

            def first_step():
                probT_lo_part(0, 2)
                base(1, 0, 1, 0)
                probT_lo_part(0, 3)
                for c in range(NC):
                    if c + 1 < NC:
                        base(1, 0, 1, c + 1)
                    score(1, 1, c)
                    negate_max(1, 1, c)
                residual(0, 0)
                dve.wait_ge(q_ok, 1)
                nc.vector.tensor_tensor(y[0][:], y[0][:], exp_h[:], ALU.add).then_inc(y_edge, 1)
                probT_lo_part(1, 0)
                row_stats(0, 0)
                probT_lo_part(1, 1)
                denominators(1, 1)
                probT_lo_part(1, 2)
                node_scores(2, 2 // NBUF, 2 % NBUF, 1)
                normalise(0, 0)
                probT_lo_part(1, 3)
                node_scores(2, 2 // NBUF, 2 % NBUF, 0)

            def step(i, r, n, layer1, prep):
                m, l, k = (n + 1) % NBUF, (n - 1) % NBUF, (n + 2) % NBUF
                rm, rk = r + (n + 1) // NBUF, r + (n + 2) // NBUF
                if not layer1 and prep:
                    return first_step()
                second = isinstance(i, int) and i == 1
                if is_graph(i - 1) and is_graph(i) and not second:
                    normalise(i - 1, l)
                if is_graph(i) and not second:
                    probT_lo_part(i, 2)
                    probT_lo_part(i, 3)
                if is_graph(i - 2) and is_graph(i - 1):
                    row_stats2(i - 2, (n - 2) % NBUF)
                if prep:
                    base(i + 1, rm, m, 0)
                    base(i + 1, rm, m, 1)
                    score(i + 1, m, 0)
                    negate_max(i + 1, m, 0)
                if is_graph(i):
                    if prep:
                        residual(i, n)
                    else:
                        last_residual(i, n)
                if prep:
                    base(i + 1, rm, m, 2)
                    score(i + 1, m, 1)
                    negate_max(i + 1, m, 1)
                    base(i + 1, rm, m, 3)
                    score(i + 1, m, 2)
                    negate_max(i + 1, m, 2)
                    score(i + 1, m, 3)
                    negate_max(i + 1, m, 3)
                if is_graph(i):
                    row_stats(i, n)
                if prep:
                    probT_lo_part(i + 1, 0)
                if is_graph(i + 2):
                    node_scores(i + 2, rk, k, 1)
                if layer1 and (prep or not is_graph(i)):
                    residual2(i - 1, l, 0)
                if prep:
                    probT_lo_part(i + 1, 1)
                if is_graph(i + 2):
                    node_scores(i + 2, rk, k, 0)
                if is_graph(i) and not prep:
                    normalise(i, n)
                if layer1:
                    for c in range(0 if is_graph(i) and not prep else 1, NC):
                        residual2(i - 1, l, c)
                        if c == 1 and is_graph(i) and not prep:
                            split_last_xn(i, n)
                if prep:
                    denominators(i + 1, m)
                if isinstance(i, int) and i == B:
                    row_stats2_end(B - 1, l)
                if isinstance(i, int) and i == B + 1:
                    normalise2_half(B - 1, (B - 1) % NBUF)

            run_steps(dve, step)

        @block.scalar
        def _(act):
            def x_hi_part(i, r, n):
                act.wait_ge(x_in[n], 16 * (r + 1))
                nc.scalar.activation(x_hi[n][:], x_sb[n][:], ACT.Copy).then_inc(x_hi_ok, 1)

            def copy_f2(i):
                act.wait_ge(f2_bcast, i + 1)
                if is_graph(i - 1):
                    act.wait_ge(neg_base_ok, NC * i)
                nc.scalar.activation(f2_row[:], ps_f2[:], ACT.Copy).then_inc(f2_row_ok, 1)

            def relu_z(i, n, c):
                if c == 0:
                    act.wait_ge(f2_row_ok, i + 1)
                    act.wait_ge(f_ok, 2 * (i + 1))
                    if is_graph(i - 1):
                        act.wait_ge(prob_ok, NC * i)
                nc.scalar.activation(score_sb[:, c, :], f2_row[:], ACT.Relu, bias=f[n][:, 0, c:c + 1],
                                     scale=(1.0 - SLOPE) / SLOPE).then_inc(relu_z_ok, 1)

            def softmax_exp(i, n, c):
                act.wait_ge(neg_max_ok, NC * i + c + 1)
                if not isinstance(i, int) or i > 0:
                    act.wait_ge(probT_ps, NC * (i - 1) + c + 1)
                nc.scalar.activation(prob[:, c, :], score_sb[:, c, :], ACT.Exp, bias=neg_max[n][:, c:c + 1], scale=1.0 / UNIT,
                                     accum_out=den[n][:, c:c + 1]).then_inc(prob_ok, 1)

            def probT_hi_part(i, c):
                act.wait_ge(probT_ps, NC * i + c + 1)
                if not isinstance(i, int) or i > 0:
                    act.wait_ge(h_ps, NC * (i - 1) + c + 1)
                nc.scalar.activation(probT_hi[:, c, :], ps_probT[c % 2][:], ACT.Copy).then_inc(probT_hi_ok, 1)

            def elu_parts(i, n, c):
                if c == 0:
                    act.wait_ge(rden_ok, i + 1)
                    if is_graph(i - 1):
                        wait_y(act, i - 1)
                act.wait_ge(h_ps, NC * i + c + 1)
                nc.scalar.activation(exp_h[:, c, :], ps_h[c % 2][:, 0:D], ACT.Exp, scale=rden[n][:, c:c + 1])
                nc.scalar.activation(y[n][:, c, :], ps_h[c % 2][:, 0:D], ACT.Relu,
                                     scale=rden[n][:, c:c + 1]).then_inc(elu_ok, 1)

            def xn_hi_part(i, n):
                act.wait_ge(xn_ok, i + 1)
                nc.scalar.activation(xn_hi[n][:], xn[n][:], ACT.Copy).then_inc(xn_hi_ok, 1)

            def scale_z(b, n, c):
                act.wait_ge(z_ps, NC * b + c + 1)
                if c == 0 and is_graph(b - 1):
                    act.wait_ge(w_ps, DC * b)
                nc.scalar.activation(z_sb[:, c, :], ps_l1[(Z0 + c) % 3][:, 0:D], ACT.Copy,
                                     scale=nrm[n][:, c:c + 1]).then_inc(z_ok, 1)

            def copy_xnT(b, d):
                act.wait_ge(xnT_ps, DC * b + d + 1)
                if d == 0 and is_graph(b - 1):
                    act.wait_ge(o_ps, NC * b)
                nc.scalar.activation(xnT[:, d, :], ps_l1[(XT0 + d) % 3][:], ACT.Copy).then_inc(xnT_ok, 1)

            def copy_w(b, d):
                act.wait_ge(w_ps, DC * b + d + 1)
                nc.scalar.activation(w_sb[:, d, :], ps_l1[(W0 + d) % 3][:, 0:D], ACT.Copy).then_inc(w_ok, 1)

            def normalise2(b, n):
                act.wait_ge(norm2_ok, b + 1)
                if is_graph(b - 1):
                    act.wait_ge(out_stored, 16 * b)
                half = isinstance(b, int) and b == B - 1
                for c in range(NC // 2 if half else NC):
                    last = nc.scalar.activation(o_sb[:, c, :], y2[n][:, c, :], ACT.Identity,
                                                bias=bias2[n][:, c:c + 1], scale=scale2[n][:, c:c + 1])
                last.then_inc(o_ok, 1)

            x_hi_part(0, 0, 0)
            copy_f2(0)
            for c in range(NC):
                relu_z(0, 0, c)
                if c == 2:
                    x_hi_part(1, 0, 1)
                if c >= 2:
                    softmax_exp(0, 0, c - 2)
            probT_hi_part(0, 0)
            softmax_exp(0, 0, 2)
            probT_hi_part(0, 1)
            softmax_exp(0, 0, 3)

            def first_step():
                probT_hi_part(0, 2)
                copy_f2(1)
                probT_hi_part(0, 3)
                for c in range(NC):
                    relu_z(1, 1, c)
                    elu_parts(0, 0, c)
                softmax_exp(1, 1, 0)
                softmax_exp(1, 1, 1)
                probT_hi_part(1, 0)
                softmax_exp(1, 1, 2)
                probT_hi_part(1, 1)
                softmax_exp(1, 1, 3)

            def step(i, r, n, layer1, prep):
                m, l = (n + 1) % NBUF, (n - 1) % NBUF
                if not layer1 and prep:
                    return first_step()
                if is_graph(i):
                    probT_hi_part(i, 2)
                    elu_parts(i, n, 0)
                    probT_hi_part(i, 3)
                if is_graph(i - 1) and is_graph(i):
                    xn_hi_part(i - 1, l)
                if is_graph(i):
                    elu_parts(i, n, 1)
                if prep:
                    copy_f2(i + 1)
                    relu_z(i + 1, m, 0)
                if is_graph(i):
                    elu_parts(i, n, 2)
                if prep:
                    relu_z(i + 1, m, 1)
                if is_graph(i):
                    elu_parts(i, n, 3)
                if prep:
                    relu_z(i + 1, m, 2)
                if layer1:
                    scale_z(i - 1, l, 0)
                    scale_z(i - 1, l, 1)
                if prep:
                    relu_z(i + 1, m, 3)
                if layer1:
                    scale_z(i - 1, l, 2)
                    scale_z(i - 1, l, 3)
                if prep:
                    x_hi_part(i + 1, r + (n + 1) // NBUF, m)
                    softmax_exp(i + 1, m, 0)
                if layer1:
                    copy_xnT(i - 1, 0)
                    copy_xnT(i - 1, 1)
                if prep:
                    softmax_exp(i + 1, m, 1)
                if layer1:
                    copy_w(i - 1, 0)
                if prep:
                    probT_hi_part(i + 1, 0)
                if layer1:
                    copy_w(i - 1, 1)
                if prep:
                    probT_hi_part(i + 1, 1)
                    softmax_exp(i + 1, m, 2)
                    softmax_exp(i + 1, m, 3)
                if is_graph(i) and not prep:
                    xn_hi_part(i, n)
                if is_graph(i - 2):
                    normalise2(i - 2, (n - 2) % NBUF)

            run_steps(act, step)

        @block.tensor
        def _(pe):
            pe.wait_ge(attn_wide_ok, 1)
            for k in range(2):
                last = nc.tensor.matmul(ps_f2[:, k * D:(k + 1) * D], attn_wide[:, k, :], wfc[:], start=True, stop=True)
            last.then_inc(ps_v_ok, 1)

            def bcast_f2(i, n):
                pe.wait_ge(f_ok, 2 * i + 1)
                if isinstance(i, int) and i == 0:
                    pe.wait_ge(consts, 3)
                else:
                    pe.wait_ge(f2_row_ok, i)
                for c in range(NC):
                    last = nc.tensor.transpose(ps_f2[:, c * P:(c + 1) * P],
                                               f[n][:, 1, c:c + 1].to_broadcast([P, P]), ident[:])
                last.then_inc(f2_bcast, 1)

            def transpose_prob(i, c):
                pe.wait_ge(prob_ok, NC * i + c + 1)
                if c >= 2:
                    pe.wait_ge(probT_lo_ok, NC * i + c - 1)
                elif not isinstance(i, int) or i > 0:
                    pe.wait_ge(probT_lo_ok, NC * i + c - 1)
                for k in range(NC):
                    last = nc.tensor.transpose(ps_probT[c % 2][:, k * P:(k + 1) * P],
                                               prob[:, c, k * P:(k + 1) * P], ident[:])
                last.then_inc(probT_ps, 1)

            def attend(i, n, c):
                pe.wait_ge(probT_lo_ok, NC * i + c + 1)
                if c == 0:
                    pe.wait_ge(x_lo_ok, i + 1)
                if c >= 2 or not isinstance(i, int) or i > 0:
                    pe.wait_ge(elu_ok, NC * i + c - 1)
                for k in range(NC):
                    blk = slice(k * P, (k + 1) * P)
                    ps = ps_h[c % 2][:, 0:D]
                    nc.tensor.matmul(ps, probT_hi[:, c, blk], x_hi[n][:, k, :], start=(k == 0), stop=False)
                    nc.tensor.matmul(ps, probT_hi[:, c, blk], x_lo[n][:, k, :], start=False, stop=False)
                    last = nc.tensor.matmul(ps, probT_lo[:, c, blk], x_hi[n][:, k, :], start=False,
                                            stop=(k == NC - 1))
                last.then_inc(h_ps, 1)

            def bank_free(b, t):
                if t >= 3:
                    u = t - 3
                    g = b
                else:
                    u = TILES + t - 3
                    g = b - 1
                    if isinstance(b, int) and b == 0:
                        return
                if u < XT0:
                    pe.wait_ge(z_ok, NC * g + u - Z0 + 1)
                elif u < W0:
                    pe.wait_ge(xnT_ok, DC * g + u - XT0 + 1)
                elif u < O0:
                    pe.wait_ge(w_ok, DC * g + u - W0 + 1)
                else:
                    pe.wait_ge(y2_ok, NC * g + u - O0 + 1)

            def make_z(b, n, c):
                bank_free(b, Z0 + c)
                if c == 0:
                    if edge(b) == 2:
                        pe.wait_ge(xn_lo_last, 1)
                    else:
                        pe.wait_ge(xn_lo_ok, b + 1)
                ps = ps_l1[(Z0 + c) % 3][:, 0:D]
                for k in range(NC):
                    a = adj_sb[n][:, k, c * P:(c + 1) * P]
                    nc.tensor.matmul(ps, a, xn_hi[n][:, k, :], start=(k == 0), stop=False)
                    last = nc.tensor.matmul(ps, a, xn_lo[n][:, k, :], start=False, stop=(k == NC - 1))
                last.then_inc(z_ps, 1)

            def transpose_xn(b, n, d):
                bank_free(b, XT0 + d)
                for c in range(NC):
                    last = nc.tensor.transpose(ps_l1[(XT0 + d) % 3][:, c * P:(c + 1) * P],
                                               xn[n][:, c, d * P:(d + 1) * P], ident[:])
                last.then_inc(xnT_ps, 1)

            def make_w(b, n, d):
                bank_free(b, W0 + d)
                ps = ps_l1[(W0 + d) % 3][:, 0:D]
                for k in range(NC):
                    if d == 0:
                        pe.wait_ge(z_ok, NC * b + k + 1)
                    last = nc.tensor.matmul(ps, z_sb[:, k, d * P:(d + 1) * P], xn[n][:, k, :], start=(k == 0),
                                            stop=(k == NC - 1))
                last.then_inc(w_ps, 1)

            def make_out(b, c):
                bank_free(b, O0 + c)
                ps = ps_l1[(O0 + c) % 3][:, 0:D]
                for d in range(DC):
                    if c == 0:
                        pe.wait_ge(xnT_ok, DC * b + d + 1)
                        pe.wait_ge(w_ok, DC * b + d + 1)
                    last = nc.tensor.matmul(ps, xnT[:, d, c * P:(c + 1) * P], w_sb[:, d, :], start=(d == 0),
                                            stop=(d == DC - 1))
                last.then_inc(o_ps, 1)

            bcast_f2(0, 0)
            transpose_prob(0, 0)
            bcast_f2(1, 1)
            transpose_prob(0, 1)
            transpose_prob(0, 2)
            transpose_prob(0, 3)

            def step(i, r, n, layer1, prep):
                m, l = (n + 1) % NBUF, (n - 1) % NBUF
                first = isinstance(i, int) and i == 0
                second = isinstance(i, int) and i == 1
                if is_graph(i) and not first:
                    transpose_prob(i, 2)
                if is_graph(i):
                    attend(i, n, 0)
                if is_graph(i) and not first:
                    transpose_prob(i, 3)
                if prep and not first and not second:
                    bcast_f2(i + 1, m)
                if is_graph(i):
                    attend(i, n, 1)
                if second:
                    bcast_f2(i + 1, m)
                if is_graph(i):
                    attend(i, n, 2)
                    attend(i, n, 3)
                if layer1:
                    for c in range(NC):
                        make_z(i - 1, l, c)
                    for d in range(DC):
                        transpose_xn(i - 1, l, d)
                    make_w(i - 1, l, 0)
                if prep:
                    transpose_prob(i + 1, 0)
                if layer1:
                    make_w(i - 1, l, 1)
                if prep:
                    transpose_prob(i + 1, 1)
                if layer1:
                    for c in range(NC):
                        make_out(i - 1, c)

            run_steps(pe, step)


def kernel(x, adj, L0_gnn_W_fc, L0_gnn_W_attn):
    import concourse.bacc as bacc
    from concourse.bass_utils import run_bass_kernel_spmd as run

    nc = bacc.Bacc("TRN2", target_bir_lowering=False, num_devices=1)
    arrays = {"x": np.ascontiguousarray(x), "adj": np.ascontiguousarray(adj),
              "w_fc": np.ascontiguousarray(L0_gnn_W_fc), "w_attn": np.ascontiguousarray(L0_gnn_W_attn)}
    ins = [nc.dram_tensor(name, a.shape, mybir.dt.from_np(a.dtype), kind="ExternalInput").ap()
           for name, a in arrays.items()]
    out = nc.dram_tensor("out", x.shape, F32, kind="ExternalOutput").ap()
    program(nc, *ins, out)
    return run(nc, [arrays], core_ids=[0]).results[0]["out"]
```
